# Optimizing a Trainium2 kernel written in Bass

```python
import numpy as np
import jax
import jax.numpy as jnp

def _softmax(x, axis=-1):
    return jax.nn.softmax(x, axis=axis)

def _gelu(x):
    return jax.nn.gelu(x, approximate=True)

def _silu(x):
    return jax.nn.silu(x)

def _sigmoid(x):
    return jax.nn.sigmoid(x)

def _layernorm(x, axis=-1, eps=1e-05):
    m = jnp.mean(x, axis=axis, keepdims=True)
    v = jnp.var(x, axis=axis, keepdims=True)
    return (x - m) / jnp.sqrt(v + eps)

def _scatter_add(tgt, idx, src, axis=0):
    return tgt.at[idx].add(src)

def _segment_sum(src, seg, n):
    return jax.ops.segment_sum(src, seg, n)
kernel_name = 'mk_flamingo_gated_d1_seqx_r4_61bade'

def setup_inputs(seed: int=0):
    np.random.seed(seed)
    _w = jnp.asarray

    def _rec_inputs():
        import jax
        import jax.numpy as jnp
        _rk = jax.random.key(seed)
        x = 0.5 + 0.2887 * jax.random.normal(jax.random.fold_in(_rk, 1), (4, 512, 512), jnp.float32)
        _lenS = 512 - jax.random.randint(jax.random.fold_in(_rk, 7), (4,), 0, max(1, 512 // 4) + 1, jnp.int32)
        _lenS2 = 512 - jax.random.randint(jax.random.fold_in(_rk, 8), (4,), 0, max(1, 512 // 4) + 1, jnp.int32)
        _ctx_512P = jax.random.normal(jax.random.fold_in(_rk, 11), (4, 16, 128), jnp.float32)
        _ctx_512c = jax.random.dirichlet(jax.random.fold_in(_rk, 511), 0.3 * jnp.ones((16,), jnp.float32), (4, 512))
        _ctx_512t = jnp.einsum('bsk,bkd->bsd', _ctx_512c, _ctx_512P)
        _ctx_512t = _ctx_512t * jax.lax.rsqrt(jnp.mean(jnp.square(_ctx_512t)) + 1e-12) * 0.953939
        ctx_512 = -0.000392918 + 0.999932 * (_ctx_512t + 0.3 * jax.random.normal(jax.random.fold_in(_rk, 611), (4, 512, 128), jnp.float32))
        _g = jax.random.normal(jax.random.fold_in(_rk, 9001), (2, 1), jnp.float32)
        _g = jnp.sign(_g) * jnp.maximum(jnp.abs(_g), 1.0) + (_g == 0) * 1.0
        g_xattn = _g[0]
        g_ffn = _g[1]
        return (x, ctx_512, g_xattn, g_ffn)
    x, ctx_512, g_xattn, g_ffn = _rec_inputs()

    def _L0_xattn_setup():
        import jax, jax.numpy as jnp
        import numpy as np
        B, N, D = (16, 512, 128)
        H = 4
        TOP_K_RATIO = 0.3
        key = jax.random.key(seed)
        k1, k2, k3, k4 = jax.random.split(key, 4)
        h = jax.random.normal(k1, (B, N, D), dtype=jnp.float32)
        adj_raw = jax.random.uniform(k2, (B, N, N), dtype=jnp.float32)
        lim = 1.0 / np.sqrt(D)
        Wq = jax.random.uniform(k3, (D, D), minval=-lim, maxval=lim, dtype=jnp.float32)
        Wk = jax.random.uniform(k4, (D, D), minval=-lim, maxval=lim, dtype=jnp.float32)
        gamma_raw = jnp.float32(-0.85)
        return {'h': h, 'adj_raw': adj_raw, 'Wq': Wq, 'Wk': Wk, 'gamma_raw': gamma_raw}
    _L0_xattn_all = _L0_xattn_setup()
    _L0_xattn_in = {k: v for k, v in _L0_xattn_all.items() if k in ('Wq', 'Wk', 'gamma_raw')}
    del _L0_xattn_all

    def _L0_ffn_setup():
        import jax, jax.numpy as jnp
        import numpy as np
        NUM_EXPERTS = 8
        HIDDEN = 512
        INTER = 512
        TOP_K = 2
        key = jax.random.key(seed)
        ks = jax.random.split(key, 7)
        hidden_states = jax.random.normal(ks[0], (4, 512, HIDDEN), dtype=jnp.float32)
        gate_w = jax.random.normal(ks[1], (HIDDEN, NUM_EXPERTS), dtype=jnp.float32) * 0.02
        fc1_w = jax.random.normal(ks[2], (NUM_EXPERTS, HIDDEN, INTER), dtype=jnp.float32) * 0.02
        fc1_b = jnp.zeros((NUM_EXPERTS, INTER), dtype=jnp.float32)
        fc2_w = jax.random.normal(ks[3], (NUM_EXPERTS, INTER, HIDDEN), dtype=jnp.float32) * 0.02
        fc2_b = jnp.zeros((NUM_EXPERTS, HIDDEN), dtype=jnp.float32)
        alpha = jax.random.normal(ks[4], (NUM_EXPERTS,), dtype=jnp.float32)
        return {'hidden_states': hidden_states, 'gate_w': gate_w, 'fc1_w': fc1_w, 'fc1_b': fc1_b, 'fc2_w': fc2_w, 'fc2_b': fc2_b, 'alpha': alpha}
    _L0_ffn_all = _L0_ffn_setup()
    _L0_ffn_in = {k: v for k, v in _L0_ffn_all.items() if k in ('gate_w', 'fc1_w', 'fc1_b', 'fc2_w', 'fc2_b', 'alpha')}
    del _L0_ffn_all
    return {'x': x, 'ctx_512': ctx_512, 'g_xattn': g_xattn, 'g_ffn': g_ffn, 'L0_xattn_Wq': _L0_xattn_in['Wq'], 'L0_xattn_Wk': _L0_xattn_in['Wk'], 'L0_xattn_gamma_raw': _L0_xattn_in['gamma_raw'], 'L0_ffn_gate_w': _L0_ffn_in['gate_w'], 'L0_ffn_fc1_w': _L0_ffn_in['fc1_w'], 'L0_ffn_fc1_b': _L0_ffn_in['fc1_b'], 'L0_ffn_fc2_w': _L0_ffn_in['fc2_w'], 'L0_ffn_fc2_b': _L0_ffn_in['fc2_b'], 'L0_ffn_alpha': _L0_ffn_in['alpha']}

def reference(x, ctx_512, g_xattn, g_ffn, L0_xattn_Wq, L0_xattn_Wk, L0_xattn_gamma_raw, L0_ffn_gate_w, L0_ffn_fc1_w, L0_ffn_fc1_b, L0_ffn_fc2_w, L0_ffn_fc2_b, L0_ffn_alpha):
    import jax
    import jax.numpy as jnp

    def _L0_xattn_ref(h, adj_raw, Wq, Wk, gamma_raw):
        import jax, jax.numpy as jnp
        import numpy as np
        B, N, D = (16, 512, 128)
        H = 4
        TOP_K_RATIO = 0.3
        b, n, dm = h.shape
        d = dm // H
        Q = (h @ Wq.T).reshape(b, n, H, d).transpose(0, 2, 1, 3)
        K = (h @ Wk.T).reshape(b, n, H, d).transpose(0, 2, 1, 3)
        sim = jnp.einsum('bhnd,bhmd->bnm', Q, K) / (jnp.sqrt(jnp.float32(d)) * H)
        k = max(1, int(n * TOP_K_RATIO))
        topk_vals = jax.lax.top_k(sim, k)[0]
        threshold = topk_vals[:, :, -1:]
        sparse_mask = (sim >= threshold).astype(sim.dtype)
        A_learned = jax.nn.sigmoid(sim) * sparse_mask
        A_learned = (A_learned + jnp.swapaxes(A_learned, -1, -2)) * 0.5
        gamma = jax.nn.sigmoid(gamma_raw)
        return (1.0 - gamma) * adj_raw + gamma * A_learned

    def _L0_ffn_ref(hidden_states, gate_w, fc1_w, fc1_b, fc2_w, fc2_b, alpha):
        import jax, jax.numpy as jnp
        import numpy as np
        NUM_EXPERTS = 8
        HIDDEN = 512
        INTER = 512
        TOP_K = 2
        B, S, H = hidden_states.shape
        x = hidden_states.reshape(-1, H)
        probs = jax.nn.softmax(x @ gate_w, axis=-1)
        gate_score, gate_idx = jax.lax.top_k(probs, TOP_K)
        gate_score = gate_score / jnp.sum(gate_score, axis=-1, keepdims=True)
        onehot = jax.nn.one_hot(gate_idx, NUM_EXPERTS, dtype=x.dtype)
        combine = jnp.einsum('tk,tke->te', gate_score, onehot) * alpha[None, :]
        h = jnp.einsum('th,ehi->eti', x, fc1_w) + fc1_b[:, None, :]
        h = jax.nn.gelu(h, approximate=False)
        y = jnp.einsum('eti,eih->eth', h, fc2_w) + fc2_b[:, None, :]
        out = jnp.einsum('eth,te->th', y, combine)
        return out.reshape(B, S, H)
    x = x + jnp.tanh(g_xattn[0]) * _L0_xattn_ref(ctx_512, _layernorm(x, axis=-1), L0_xattn_Wq, L0_xattn_Wk, L0_xattn_gamma_raw)
    x = x + jnp.tanh(g_ffn[0]) * _L0_ffn_ref(_layernorm(x, axis=-1), L0_ffn_gate_w, L0_ffn_fc1_w, L0_ffn_fc1_b, L0_ffn_fc2_w, L0_ffn_fc2_b, L0_ffn_alpha)
    return x

_drawn_inputs = setup_inputs


def setup_inputs(seed=0):
    import zlib

    import numpy as np

    out = dict(_drawn_inputs(seed))
    spreads = {'L0_ffn_fc1_b': (0.0, 0.424), 'L0_ffn_fc2_b': (0.0, 0.1)}
    factors = {}
    for name, (base, spread) in spreads.items():
        noise = np.random.default_rng([zlib.crc32(name.encode()), seed]).standard_normal(out[name].shape)
        drawn = base * np.exp(spread * noise) if base else spread * noise
        out[name] = jnp.asarray(drawn.astype(out[name].dtype))
    for name, factor in factors.items():
        out[name] = (out[name] * factor).astype(out[name].dtype)
    return out
```

```python
from contextlib import ExitStack

import concourse.bass as bass
import numpy as np
from concourse import mybir

F32 = mybir.dt.float32
BF16 = mybir.dt.bfloat16
I32 = mybir.dt.int32
U32 = mybir.dt.uint32
ALU = mybir.AluOpType
ACT = mybir.ActivationFunctionType
AX = mybir.AxisListType

P = 128
BATCH, SEQ, D = 4, 512, 512
C = 128
HEADS = 4
E = 8
PICKS = 2
INTER = 512
TOKENS = BATCH * SEQ
T = TOKENS // P
BT = SEQ // P
KB = D // P
IB = INTER // P
TOPK = int(SEQ * 0.3)
GROUPS = T * PICKS
TILES = (TOKENS * PICKS + E * (P - 1)) // P
LN_EPS = 1e-5
SIM_SCALE = float(np.float32(1.0) / (np.sqrt(np.float32(C // HEADS)) * np.float32(HEADS)))

ROUNDS = 6
T_DVE = 9
WINDOW = 8
AIM = TOPK - WINDOW / 2
START_SIGMAS = 0.55
DENSITY = 0.35
BRACKET_LOW, BRACKET_HIGH = 3.0, 3.5
BIG = 1e30
LOWEST = -3e38
RSQRT_MAGIC = 1597463007.0


def build(nc, x, ctx_in, g_x, g_f, wq_in, wk_in, gam_in, gate_in, fc1, b1_in, fc2, b2_in, alpha_in, xn_rows, out_rows):
    es = ExitStack()
    with es:
        def sb(name, shape, dt=F32):
            return es.enter_context(nc.sbuf_tensor(name, shape, dt))

        def sem(name):
            return es.enter_context(nc.semaphore(name))

        weights = sb("weights", [P, E, 2, KB, INTER])
        sim = sb("sim", [P, T, SEQ])
        xb = sb("xb", [P, 2, BT, D])
        ab = sb("ab", [P, 2, BT, SEQ])
        xnb = sb("xnb", [P, BT, D])
        xnT = sb("xnT", [P, 2, D])
        ab_flat = ab[:].rearrange("p u t n -> p (u t n)")
        sim_flat = sim[:].rearrange("p t n -> p (t n)")
        ctx_b = [ab_flat[:, u * 2048:u * 2048 + 512] for u in range(2)]
        ctxT = [ab_flat[:, u * 2048 + 512:u * 2048 + 1024] for u in range(2)]
        qT = [ab_flat[:, u * 2048 + 1024:u * 2048 + 1536] for u in range(2)]
        kT = [ab_flat[:, u * 2048 + 1536:u * 2048 + 2048] for u in range(2)]
        slot_hot = sim_flat[:, 0:GROUPS * P].rearrange("p (g q) -> p g q", g=GROUPS)
        tile_hot = ab_flat[:, 0:GROUPS * 3 * TILES].rearrange("p (g v j) -> p g v j", g=GROUPS, v=3)
        b2_bc = xb[:].rearrange("p u t n -> p (u t n)").rearrange("p (e n) -> p e n", e=E)

        def ring(at, n=2):
            return [sim_flat[:, (at + u) * 512:(at + u + 1) * 512] for u in range(n)]

        xg, xgT, hid, act_t, yb, ys = ring(0), ring(2), ring(4), ring(6), ring(8), ring(10)

        xnb_flat = xnb[:].rearrange("p t n -> p (t n)")
        wq, wk, wqT, wkT = (xnb_flat[:, n * C:(n + 1) * C] for n in range(4))
        b1_rows = xnb_flat[0:E * IB, 512:640]
        junk = ab_flat.bitcast(BF16).rearrange("p (i n) -> p i n", i=T)
        hot = sim_flat[:, 6144:6400].rearrange("p (i k e) -> p i k e", k=PICKS, e=E)
        hot_w = sim_flat[:, 6400:6656].rearrange("p (i k e) -> p i k e", k=PICKS, e=E)
        totals, running, tiles_cmp = (sim_flat[:, at:at + T * E].rearrange("p (e i) -> p e i", e=E) for at in (6656, 6784, 6912))
        place = sim_flat[:, 7040:7168].rearrange("p (i e) -> p i e", e=E)

        exp_cmp = sim_flat[0:1, 7168:7168 + TILES * E].rearrange("p (j e) -> p j e", e=E)
        table = sim_flat[:, 7488:7488 + 3 * TILES].rearrange("p (v j) -> p v j", v=3)
        top, pick = (ab_flat[:, at:at + T * WINDOW].rearrange("p (i w) -> p i w", w=WINDOW) for at in (0, 128))
        pad_zero = xnb_flat[:, 1536:1536 + D]

        ident = sb("ident", [P, P])
        ident_a = sb("ident_a", [P, P])
        before = sb("before", [P, P], BF16)
        ones_b = sb("ones_b", [P, P], BF16)
        ones = sb("ones", [P, T * E])
        gate_w = sb("gate_w", [P, KB, E])
        b1T = sb("b1T", [P, E * IB])
        raw = sb("raw", [P, 3])
        alpha_bc = sb("alpha_bc", [P, E])
        coef = sb("coef", [P, 8])
        iota_e = sb("iota_e", [P, E])
        iota_q = sb("iota_q", [P, P])
        iota_j = sb("iota_j", [P, TILES])
        tile_starts = sb("tile_starts", [P, T])
        token_id = sb("token_id", [P, T])
        pad_row = sb("pad_row", [P, 1])

        stats = sb("stats", [P, T, 6])
        mv = sb("mv", [P, T, 2])
        dev = sb("dev", [P, T])
        t_now = sb("t_now", [P, T])
        t_neg = sb("t_neg", [P, T])
        cnt = sb("cnt", [P, T])
        lo = sb("lo", [P, T])
        hi = sb("hi", [P, T])
        c_lo = sb("c_lo", [P, T])
        c_hi = sb("c_hi", [P, T])
        over = sb("over", [P, T], I32)
        under = sb("under", [P, T], I32)
        tmp0 = sb("tmp0", [P, T])
        tmp1 = sb("tmp1", [P, T])
        thr = sb("thr", [P, T])
        bad = sb("bad", [P, 1])
        bad_i = sb("bad_i", [1, 1], I32)
        work = sb("work", [P, 8])

        statx = sb("statx", [P, 2, BT, 6])
        mvx = sb("mvx", [P, 2, BT, 2])
        rstd = sb("rstd", [P, 2, BT])
        nt0 = sb("nt0", [P, BT])
        nt1 = sb("nt1", [P, BT])
        nti = sb("nti", [P, BT], I32)
        xa_scale = sb("xa_scale", [P, BT])
        xa_bias = sb("xa_bias", [P, BT])
        xn_scale = sb("xn_scale", [P, BT])
        xn_bias = sb("xn_bias", [P, BT])

        logits = sb("logits", [P, BT, E])
        best = sb("best", [P, BT, E])
        best_i = sb("best_i", [P, BT, E], U32)
        idx_f = sb("idx_f", [P, T, PICKS])
        member = sb("member", [P, T * E], BF16)
        gap = sb("gap", [P, T])
        score = sb("score", [P, T, PICKS])
        w_tok = sb("w_tok", [P, T, PICKS])
        count_e = sb("count_e", [P, E])
        start_e = sb("start_e", [P, E])
        tiles_e = sb("tiles_e", [P, E])
        tiles_end = sb("tiles_end", [P, E])
        base_e = sb("base_e", [P, E])
        pos = sb("pos", [P, GROUPS])
        pos_i = sb("pos_i", [P, GROUPS], I32)
        pos_q = sb("pos_q", [P, GROUPS], I32)
        pos_j = sb("pos_j", [P, GROUPS], I32)
        pos_qf = sb("pos_qf", [P, GROUPS])
        pos_jf = sb("pos_jf", [P, GROUPS])
        exp_f = sb("exp_f", [1, TILES])
        exp_i = sb("exp_i", [1, TILES], I32)
        w_slot = sb("w_slot", [P, TILES])
        src_idx = sb("src_idx", [P, TILES + 1], U32)
        dst_idx = sb("dst_idx", [P, TILES], U32)

        src_now = sb("src_now", [P, 2], U32)
        dst_now = sb("dst_now", [P, 2], U32)

        ps = es.enter_context(nc.psum_tensor("ps", [P, 8, 512], F32))

        const_in, qk_in, b1_in_s, scal_in = sem("const_in"), sem("qk_in"), sem("b1_in_s"), sem("scal_in")
        ctx_in_s = [sem("ctx_in0"), sem("ctx_in1")]
        x_in = [sem("x_in0"), sem("x_in1")]
        fc1_in, fc2_in, b2_in_s = sem("fc1_in"), sem("fc2_in"), sem("b2_in_s")
        consts = sem("consts")
        wT_ps, wT_sb = sem("wT_ps"), sem("wT_sb")
        coef_ok = sem("coef_ok")
        ctxT_ps, ctxT_sb, q_ps, q_sb, k_ps, k_sb = (sem(n) for n in ("ctxT_ps", "ctxT_sb", "q_ps", "q_sb", "k_ps", "k_sb"))
        sim_ps, sim_sb = sem("sim_ps"), sem("sim_sb")
        trial, counted, pen_done, pen_used = sem("trial"), sem("counted"), sem("pen_done"), sem("pen_used")
        bad_sb, bad_ps, thr_ok = sem("bad_sb"), sem("bad_ps"), sem("thr_ok")
        act_coef, sig_done, a_done, xa_done = sem("act_coef"), sem("sig_done"), sem("a_done"), sem("xa_done")
        x1_ps, x1_sb, xn_coef, xn_done = (sem(n) for n in ("x1_ps", "x1_sb", "xn_coef", "xn_done"))
        xnT_ps, xnT_sb, log_ps, log_sb = sem("xnT_ps"), sem("xnT_sb"), sem("log_ps"), sem("log_sb")
        xn_out, x1_out, pad_out = sem("xn_out"), sem("x1_out"), sem("pad_out")
        gap_ok, score_ok, member_ok, rank_ps, hot_ok, table_ps, route_ok, slots_ok = (
            sem(n) for n in ("gap_ok", "score_ok", "member_ok", "rank_ps", "hot_ok", "table_ps", "route_ok", "slots_ok"))
        src_set, dst_set, pool_turn, rows_added = sem("src_set"), sem("dst_set"), sem("pool_turn"), sem("rows_added")
        gathered = [sem("gathered0"), sem("gathered1")]
        scattered = [sem("scattered0"), sem("scattered1")]
        xgT_ps, xgT_sb, hid_ps, hid_sb, hidT_ps, gelu_sb, y_ps, y_sb, ys_ready = (
            sem(n) for n in ("xgT_ps", "xgT_sb", "hid_ps", "hid_sb", "hidT_ps", "gelu_sb", "y_ps", "y_sb", "ys_ready"))

        ctx_v = ctx_in.rearrange("(b t p) c -> b p t c", t=BT, p=P)
        x_v = x.rearrange("(b t p) n -> b p t n", t=BT, p=P)
        xn_v = xn_rows.rearrange("(b t p) n -> b p t n", t=BT, p=P)
        out_v = out_rows[0:TOKENS, :].rearrange("(b t p) n -> b p t n", t=BT, p=P)

        def bc_row(v, n):
            return v.rearrange("(a b) -> a b", a=1).to_broadcast([P, n])

        block = es.enter_context(nc.Block())

        @block.sync
        def _(sp):
            sp.dma_start(wq, wq_in).then_inc(qk_in, 16)
            sp.dma_start(wk, wk_in).then_inc(qk_in, 16)
            for u in range(2):
                sp.dma_start(ctx_b[u].rearrange("p (t c) -> p t c", t=BT), ctx_v[u]).then_inc(ctx_in_s[u], 16)
            for n, g in enumerate((g_x, g_f, gam_in)):
                sp.dma_start(raw[:, n:n + 1], bc_row(g, 1)).then_inc(scal_in, 16)
            sp.dma_start(alpha_bc[:], bc_row(alpha_in, E)).then_inc(scal_in, 16)
            sp.dma_start(b1_rows, b1_in.rearrange("e (i p) -> (e i) p", p=P)).then_inc(b1_in_s, 16)
            sp.dma_start(gate_w[:], gate_in.rearrange("(k p) e -> p k e", p=P)).then_inc(const_in, 16)
            for u in range(2):
                sp.dma_start(xb[:, u], x_v[u]).then_inc(x_in[u], 16)
            for u in range(2):
                sp.wait_ge(ctxT_ps, u + 1)
                sp.dma_start(ctx_b[u].rearrange("p (t c) -> p t c", t=BT), ctx_v[2 + u]).then_inc(ctx_in_s[u], 16)
            sp.wait_ge(consts, 1)
            sp.dma_start(out_rows[TOKENS:TOKENS + P, :], pad_zero).then_inc(pad_out, 16)
            for b in range(BATCH):
                u = b % 2
                sp.wait_ge(x1_sb, BT + BT * (b + 1))
                sp.dma_start(out_v[b], xb[:, u]).then_inc(x1_out, 16)
                sp.wait_ge(xn_done, BT * (b + 1))
                sp.dma_start(xn_v[b], xnb[:]).then_inc(xn_out, 16)
                if b + 2 < BATCH:
                    sp.wait_ge(x1_out, 16 * (b + 1))
                    sp.dma_start(xb[:, u], x_v[b + 2]).then_inc(x_in[u], 16)
            sp.wait_ge(x1_out, 16 * BATCH)
            sp.dma_start(b2_bc, b2_in.rearrange("(a e) n -> a e n", a=1).to_broadcast([P, E, D])).then_inc(b2_in_s, 16)

        @block.gpsimd
        def _(pool):
            pool.memset(pad_zero, 0.0).then_inc(consts, 1)
            pool.memset(ident[:], 0.0)
            pool.memset(ones_b[:], 1.0)
            pool.memset(ones[:], 1.0)
            pool.drain()
            pool.affine_select(out=ident[:], in_=ident[:], compare_op=ALU.not_equal, fill=1.0, base=0,
                               pattern=[[-1, P]], channel_multiplier=1).then_inc(consts, 1)
            pool.affine_select(out=before[:], in_=ones_b[:], compare_op=ALU.is_gt, fill=0.0, base=0,
                               pattern=[[1, P]], channel_multiplier=-1)
            for buf, pattern, base, by in (
                (iota_e[:], [[1, E]], 0, 0), (iota_q[:], [[1, P]], 0, 0), (iota_j[:], [[1, TILES]], 0, 0),
                (tile_starts[:], [[P, T]], 0, 0), (token_id[:], [[P, T]], 0, 1), (pad_row[:], [[1, 1]], TOKENS, 1),
            ):
                pool.iota(buf, pattern, base=base, channel_multiplier=by, allow_small_or_imprecise_dtypes=True)
            pool.memset(src_idx[:], 0)
            pool.drain().then_inc(consts, 1)

            pool.wait_ge(xn_out, 16 * BATCH + 16)
            pool.wait_ge(x1_out, 16 * BATCH)
            pool.wait_ge(pad_out, 16)
            pool.wait_ge(slots_ok, 1)

            last_token, last_row = pool.to_reg(TOKENS - 1), pool.to_reg(TOKENS + P - 1)

            def gather(j, u):
                pool.tensor_copy(src_now[:, u:u + 1], src_idx[:, bass.ds(j, 1)]).then_inc(src_set, 1)
                pool.wait_ge(src_set, j + 1)
                pool.sem_inc(pool_turn, 1)
                pool.indirect_dma_start(
                    out=xg[u], out_offset=None, in_=xn_rows,
                    in_offset=bass.IndirectOffsetOnAxis(ap=src_now[:, u:u + 1], axis=0),
                    bounds_check=last_token).then_inc(gathered[u], 16)

            def scatter(j, u, scatters):
                pool.tensor_copy(dst_now[:, u:u + 1], dst_idx[:, bass.ds(j, 1)]).then_inc(dst_set, 1)
                pool.wait_ge(dst_set, j + 1)
                pool.wait_ge(ys_ready, j + 1)
                pool.sem_inc(pool_turn, 1)
                pool.indirect_dma_start(
                    out=out_rows, out_offset=bass.IndirectOffsetOnAxis(ap=dst_now[:, u:u + 1], axis=0),
                    in_=ys[u], in_offset=None, bounds_check=last_row,
                    compute_op=ALU.add).then_inc(scattered[u], 16)
                pool.wait_ge(scattered[u], scatters)
                pool.sem_inc(rows_added, 1)

            gather(0, 0)
            gather(1, 1)
            with pool.Fori(0, (TILES - 1) // 2) as jj:
                for u in range(2):
                    j = jj * 2 + u
                    pool.wait_ge(xgT_ps, j + 1)
                    gather(j + 2, u)
                    scatter(j, u, 16 * jj + 16)
            scatter(TILES - 1, 0, 16 * ((TILES + 1) // 2))
            pool.wait_ge(gathered[1], 16 * ((TILES - 1) // 2 + 1))

        @block.scalar
        def _(act):
            act.sem_inc(sim_sb, 2 * BT)
            act.sem_inc(x1_sb, BT)
            act.wait_ge(scal_in, 64)
            act.activation(coef[:, 0:2], raw[:, 0:2], ACT.Tanh)
            act.activation(coef[:, 2:3], raw[:, 2:3], ACT.Sigmoid).then_inc(act_coef, 1)
            act.wait_ge(qk_in, 32)
            act.wait_ge(wT_ps, 1)
            act.copy(wqT, ps[:, 3, 0:C])
            act.copy(wkT, ps[:, 3, C:2 * C])
            act.copy(b1T[:], ps[:, 3, 2 * C:2 * C + E * IB])
            act.drain().then_inc(wT_sb, 1)
            for e in range(E):
                for m, (fc, s) in enumerate(((fc1, fc1_in), (fc2, fc2_in))):
                    act.dma_start(weights[:, e, m], fc[e].rearrange("(k p) n -> p k n", p=P)).then_inc(s, 16)
            with act.Fori(0, 2) as h:
                for u in range(2):
                    b = h * 2 + u
                    act.wait_ge(ctxT_ps, b + 1)
                    act.copy(ctxT[u], ps[:, 4 * u, :]).then_inc(ctxT_sb, 1)
                    act.wait_ge(k_ps, b + 1)
                    act.copy(kT[u], ps[:, 4 * u + 2, :]).then_inc(k_sb, 1)
                    for t in range(BT):
                        act.wait_ge(sim_ps, b * BT + t + 1)
                        act.activation(sim[:, bass.ds(b * BT + t, 1), :].rearrange("p a n -> p (a n)"),
                                       ps[:, 4 * u + t, :], ACT.Copy, scale=SIM_SCALE).then_inc(sim_sb, 1)
            act.drain()

            def sign_sums():
                for i in range(T_DVE, T):
                    last = act.activation(junk[:, i, :], sim[:, i, :], ACT.Sign, bias=t_neg[:, i:i + 1],
                                          accum_out=cnt[:, i:i + 1])
                last.then_inc(counted, 1)
                act.drain()

            with act.Fori(0, ROUNDS) as r:
                act.wait_ge(trial, r + 1)
                sign_sums()
            act.wait_ge(trial, ROUNDS + 1)
            for i in range(T):
                if i >= 2:
                    act.wait_ge(pen_used, i - 1)
                act.activation(xnT[:, i % 2, :], sim[:, i, :], ACT.Relu, bias=t_neg[:, i:i + 1],
                               scale=BIG).then_inc(pen_done, 1)
            act.wait_ge(trial, ROUNDS + 2)
            sign_sums()
            act.wait_ge(bad_sb, 1)
            act.wait_ge(pad_out, 16)
            with act.Fori(0, 2) as h:
                for u in range(2):
                    b = h * 2 + u
                    act.wait_ge(x1_ps, b * BT + BT)
                    for t in range(BT):
                        act.activation(ab[:, u, t, :], sim[:, bass.ds(b * BT + t, 1), :].rearrange("p a n -> p (a n)"),
                                       ACT.Sigmoid).then_inc(sig_done, 1)
                    act.wait_ge(coef_ok, b + 2)
                    for t in range(BT):
                        act.activation(xb[:, u, t, :], xb[:, u, t, :], ACT.Identity, scale=xa_scale[:, t:t + 1],
                                       bias=xa_bias[:, t:t + 1]).then_inc(xa_done, 1)
                    for t in range(BT):
                        act.wait_ge(x1_ps, 2 * BT + b * BT + t + 1)
                        act.copy(xb[:, u, t, :], ps[:, t, :]).then_inc(x1_sb, 1)
                    act.drain()
                    act.wait_ge(xn_coef, b + 1)
                    act.wait_ge(xn_out, b * 16 + 16)
                    act.wait_ge(xnT_ps, b * BT + 4)
                    for t in range(BT):
                        act.activation(xnb[:, t, :], xb[:, u, t, :], ACT.Identity, scale=xn_scale[:, t:t + 1],
                                       bias=xn_bias[:, t:t + 1]).then_inc(xn_done, 1)
            act.wait_ge(gap_ok, 1)
            act.activation(score[:, :, 0], gap[:], ACT.Sigmoid)
            act.activation(score[:, :, 1], gap[:], ACT.Sigmoid, scale=-1.0).then_inc(score_ok, 1)

            act.wait_ge(route_ok, 1)

            def gelu(j, u):
                e = act.value_load(exp_i[0:1, bass.ds(j, 1)], min_val=0, max_val=E - 1)
                act.wait_ge(hidT_ps, j + 1)
                for i in range(IB):
                    last = act.activation(act_t[u][:, i * P:(i + 1) * P], ps[:, 4 + u, i * P:(i + 1) * P], ACT.Gelu,
                                          bias=b1T[:, bass.ds(e * IB + i, 1)])
                last.then_inc(gelu_sb, 1)

            with act.Fori(0, (TILES - 1) // 2) as jj:
                for u in range(2):
                    gelu(jj * 2 + u, u)
            gelu(TILES - 1, 0)

        @block.vector
        def _(dve):
            dve.wait_ge(act_coef, 1)
            dve.tensor_scalar(coef[:, 5:6], coef[:, 2:3], -1.0, 1.0, ALU.mult, ALU.add)
            dve.tensor_scalar(coef[:, 4:5], coef[:, 2:3], coef[:, 0:1], 0.5, ALU.mult, ALU.mult)
            dve.drain()
            dve.tensor_tensor(coef[:, 3:4], coef[:, 5:6], coef[:, 0:1], ALU.mult)
            dve.wait_ge(consts, 3)
            dve.tensor_scalar(ident_a[:], ident[:], coef[:, 4:5], None, ALU.mult)
            dve.drain().then_inc(coef_ok, 1)
            dve.sem_inc(x1_ps, 2 * BT)
            dve.sem_inc(xn_out, 16)
            dve.sem_inc(xnT_ps, BT)
            dve.sem_inc(log_sb, 1)
            dve.sem_inc(y_sb, 2)
            dve.sem_inc(rows_added, 2)

            with dve.Fori(0, 2) as h:
                for u in range(2):
                    b = h * 2 + u
                    dve.wait_ge(q_ps, b + 1)
                    dve.tensor_copy(qT[u], ps[:, 4 * u + 1, :]).then_inc(q_sb, 1)
                    for t in range(BT):
                        dve.wait_ge(sim_sb, 2 * BT + b * BT + t + 1)
                        dve.bn_stats(stats[:, bass.ds(b * BT + t, 1), :].rearrange("p a n -> p (a n)"),
                                     sim[:, bass.ds(b * BT + t, 1), :].rearrange("p a n -> p (a n)"))
            dve.drain()
            for i in range(T):
                dve.bn_aggr(mv[:, i, :], stats[:, i, :])
            dve.drain()
            mean, var = mv[:, :, 0], mv[:, :, 1]

            def rsqrt(y, v, a, b, bits, shape_src):
                dve.tensor_scalar(bits, shape_src, 1, None, ALU.logical_shift_right)
                dve.drain()
                dve.tensor_scalar(y.bitcast(I32), bits, -1.0, RSQRT_MAGIC, ALU.mult, ALU.add)
                dve.drain()
                for _ in range(3):
                    dve.scalar_tensor_tensor(a, y, -0.5, y, ALU.mult, ALU.mult)
                    dve.drain()
                    dve.tensor_tensor(b, a, v, ALU.mult)
                    dve.drain()
                    dve.scalar_tensor_tensor(y, b, 1.5, y, ALU.add, ALU.mult)
                    dve.drain()

            dve.tensor_scalar(tmp0[:], var, 1e-30, None, ALU.max)
            dve.drain()
            rsqrt(tmp1[:], tmp0[:], lo[:], hi[:], over[:], tmp0[:].bitcast(I32))
            dve.tensor_tensor(dev[:], tmp0[:], tmp1[:], ALU.mult)
            dve.drain()
            dve.scalar_tensor_tensor(t_now[:], dev[:], START_SIGMAS, mean, ALU.mult, ALU.add)
            dve.scalar_tensor_tensor(lo[:], dev[:], -BRACKET_LOW, mean, ALU.mult, ALU.add)
            dve.scalar_tensor_tensor(hi[:], dev[:], BRACKET_HIGH, mean, ALU.mult, ALU.add)
            dve.memset(c_lo[:], float(SEQ))
            dve.memset(c_hi[:], 0.0)

            def publish(scale=-1.0, of=t_now):
                dve.drain()
                dve.tensor_scalar(t_neg[:], of[:], scale, None, ALU.mult)
                dve.drain().then_inc(trial, 1)

            def count(rounds, half):
                for i in range(T_DVE):
                    dve.tensor_scalar(junk[:, i, :], sim[:, i, :], t_now[:, i:i + 1], None, ALU.is_ge, ALU.add,
                                      accum_out=cnt[:, i:i + 1])
                dve.wait_ge(counted, rounds)
                dve.tensor_scalar(cnt[:, T_DVE:T], cnt[:, T_DVE:T], 0.5, SEQ / 2 + half, ALU.mult, ALU.add)
                dve.drain()

            def narrow():
                dve.tensor_scalar(over[:], cnt[:], float(TOPK), None, ALU.is_ge)
                dve.tensor_scalar(under[:], cnt[:], float(TOPK), None, ALU.is_lt)
                dve.drain()
                dve.copy_predicated(lo[:], over[:], t_now[:])
                dve.copy_predicated(c_lo[:], over[:], cnt[:])
                dve.copy_predicated(hi[:], under[:], t_now[:])
                dve.copy_predicated(c_hi[:], under[:], cnt[:])
                dve.drain()

            publish()
            count(1, 0.0)
            narrow()
            dve.tensor_scalar(tmp0[:], cnt[:], -AIM, 1.0 / (SEQ * DENSITY), ALU.add, ALU.mult)
            dve.drain()
            dve.tensor_tensor(tmp1[:], tmp0[:], dev[:], ALU.mult)
            dve.drain()
            dve.tensor_tensor(t_now[:], t_now[:], tmp1[:], ALU.add)
            publish()
            with dve.Fori(1, ROUNDS - 1) as r:
                count(r + 1, 0.0)
                narrow()
                dve.tensor_tensor(tmp0[:], c_lo[:], c_hi[:], ALU.subtract)
                dve.tensor_scalar(tmp1[:], c_hi[:], -1.0, AIM, ALU.mult, ALU.add)
                dve.drain()
                dve.reciprocal(tmp0[:], tmp0[:])
                dve.drain()
                dve.tensor_tensor(tmp0[:], tmp0[:], tmp1[:], ALU.mult)
                dve.drain()
                dve.tensor_scalar(tmp0[:], tmp0[:], 0.05, 0.95, ALU.max, ALU.min)
                dve.tensor_tensor(tmp1[:], lo[:], hi[:], ALU.subtract)
                dve.drain()
                dve.tensor_tensor(tmp1[:], tmp1[:], tmp0[:], ALU.mult)
                dve.drain()
                dve.tensor_tensor(t_now[:], tmp1[:], hi[:], ALU.add)
                publish()
            count(ROUNDS, 0.0)
            narrow()
            publish(-BIG, hi)
            for i in range(T):
                dve.wait_ge(pen_done, i + 1)
                dve.tensor_tensor(xnT[:, i % 2, :], sim[:, i, :], xnT[:, i % 2, :], ALU.subtract)
                dve.drain()
                dve.max(out=top[:, i, :], in_=xnT[:, i % 2, :]).then_inc(pen_used, 1)
            dve.tensor_scalar(tmp0[:], c_hi[:], -1.0, float(TOPK - 1), ALU.mult, ALU.add)
            dve.drain()
            dve.tensor_tensor(pick, iota_e[:, None, :].to_broadcast([P, T, WINDOW]),
                              tmp0[:, :, None].to_broadcast([P, T, WINDOW]), ALU.is_equal)
            dve.drain()
            dve.tensor_tensor(pick, pick, top, ALU.mult)
            dve.drain()
            dve.tensor_reduce(t_now[:], pick, AX.X, ALU.add)
            publish()
            dve.tensor_copy(thr[:], t_now[:])
            count(ROUNDS + 1, 0.5)
            dve.tensor_scalar(tmp0[:], cnt[:], float(TOPK), None, ALU.not_equal, ALU.add, accum_out=bad[:])
            dve.drain().then_inc(bad_sb, 1)
            dve.wait_ge(bad_ps, 1)
            dve.tensor_copy(bad_i[:], ps[0:1, 7, 0:1])
            dve.drain()
            unproved = dve.value_load(bad_i[0:1, 0:1], min_val=0, max_val=TOKENS)
            with dve.If(unproved > 0):
                with dve.Fori(0, T) as i:
                    dve.tensor_copy(xnT[:, 0, :], sim[:, bass.ds(i, 1), :].rearrange("p a n -> p (a n)"))
                    dve.drain()
                    with dve.Fori(0, (TOPK - 1) // WINDOW):
                        dve.max(out=work[:], in_=xnT[:, 0, :])
                        dve.drain()
                        dve.match_replace(out=xnT[:, 0, :], in_to_replace=work[:], in_values=xnT[:, 0, :],
                                          imm_value=LOWEST)
                        dve.drain()
                    dve.max(out=work[:], in_=xnT[:, 0, :])
                    dve.drain()
                    dve.tensor_copy(thr[:, bass.ds(i, 1)], work[:, (TOPK - 1) % WINDOW:(TOPK - 1) % WINDOW + 1])
                    dve.drain()
            with dve.Else():
                dve.drain()
            dve.drain()

            def norm(n):
                dve.tensor_scalar(nt0[:], mvx[:, n, :, 1], LN_EPS, None, ALU.add)
                dve.drain()
                dve.tensor_copy(mvx[:, n, :, 1], nt0[:])
                dve.drain()
                rsqrt(rstd[:, n, :], mvx[:, n, :, 1], nt0[:], nt1[:], nti[:], nt0[:].bitcast(I32))

            with dve.Fori(0, 2) as h:
                for u in range(2):
                    b = h * 2 + u
                    dve.wait_ge(x_in[u], 16 * h + 16)
                    for t in range(BT):
                        dve.bn_stats(statx[:, 0, t, :], xb[:, u, t, :])
                    dve.drain()
                    for t in range(BT):
                        dve.bn_aggr(mvx[:, 0, t, :], statx[:, 0, t, :])
                    dve.drain()
                    norm(0)
                    dve.tensor_scalar(nt0[:], rstd[:, 0, :], coef[:, 3:4], None, ALU.mult)
                    dve.drain()
                    dve.tensor_scalar(xa_scale[:], nt0[:], 1.0, None, ALU.add)
                    dve.scalar_tensor_tensor(xa_bias[:], nt0[:], -1.0, mvx[:, 0, :, 0], ALU.mult, ALU.mult)
                    dve.drain().then_inc(coef_ok, 1)
                    for t in range(BT):
                        dve.wait_ge(sig_done, b * BT + t + 1)
                        dve.scalar_tensor_tensor(
                            ab[:, u, t, :], sim[:, bass.ds(b * BT + t, 1), :].rearrange("p a n -> p (a n)"),
                            thr[:, bass.ds(b * BT + t, 1)], ab[:, u, t, :], ALU.is_ge, ALU.mult).then_inc(a_done, 1)
                    for t in range(BT):
                        dve.wait_ge(x1_sb, BT + b * BT + t + 1)
                        dve.bn_stats(statx[:, 1, t, :], xb[:, u, t, :])
                    dve.drain()
                    for t in range(BT):
                        dve.bn_aggr(mvx[:, 1, t, :], statx[:, 1, t, :])
                    dve.drain()
                    norm(1)
                    dve.scalar_tensor_tensor(xn_bias[:], rstd[:, 1, :], -1.0, mvx[:, 1, :, 0], ALU.mult, ALU.mult)
                    dve.tensor_copy(xn_scale[:], rstd[:, 1, :])
                    dve.drain().then_inc(xn_coef, 1)
                    for t in range(BT):
                        dve.wait_ge(xnT_ps, b * BT + t + 5)
                        dve.tensor_copy(xnT[:, t % 2, :], ps[:, 4 + t % 2, :]).then_inc(xnT_sb, 1)
                    dve.wait_ge(log_ps, b + 1)
                    dve.tensor_copy(logits[:], ps[:, 6, 0:BT * E].rearrange("p (t e) -> p t e", t=BT))
                    dve.drain().then_inc(log_sb, 1)
                    for t in range(BT):
                        dve.max(out=best[:, t, :], in_=logits[:, t, :])
                    dve.drain()
                    for t in range(BT):
                        dve.max_index(out=best_i[:, t, :], in_max=best[:, t, :], in_values=logits[:, t, :])
                    dve.tensor_tensor(gap[:, bass.ds(b * BT, BT)], best[:, :, 0], best[:, :, 1], ALU.subtract)
                    dve.drain()
                    dve.tensor_copy(idx_f[:, bass.ds(b * BT, BT), :], best_i[:, :, 0:PICKS])
            dve.drain().then_inc(gap_ok, 1)
            hot_g = hot.rearrange("p i k e -> p (i k) e")
            hot_wg = hot_w.rearrange("p i k e -> p (i k) e")
            dve.tensor_tensor(hot_g, iota_e[:, None, :].to_broadcast([P, GROUPS, E]),
                              idx_f[:].rearrange("p i k -> p (i k)")[:, :, None].to_broadcast([P, GROUPS, E]), ALU.is_equal)
            dve.drain()
            dve.tensor_tensor(member[:].rearrange("p (i e) -> p i e", i=T), hot[:, :, 0, :], hot[:, :, 1, :], ALU.add)
            dve.drain().then_inc(member_ok, 1)
            dve.tensor_tensor(hot_wg, hot_g, alpha_bc[:, None, :].to_broadcast([P, GROUPS, E]), ALU.mult)
            dve.drain()
            w_g = w_tok[:].rearrange("p i k -> p (i k)")
            dve.tensor_reduce(w_g, hot_wg, AX.X, ALU.add)
            dve.drain()
            dve.wait_ge(score_ok, 1)
            dve.scalar_tensor_tensor(w_g, score[:].rearrange("p i k -> p (i k)"), coef[:, 1:2], w_g, ALU.mult, ALU.mult)
            dve.wait_ge(rank_ps, 1)
            dve.tensor_copy(totals, ps[:, 5, 0:T * E].rearrange("p (i e) -> p e i", i=T))
            dve.drain()
            tot_f = totals.rearrange("p e i -> p (e i)")
            run_f = running.rearrange("p e i -> p (e i)")
            dve.tensor_tensor_scan(out=run_f, data0=ones[:], data1=tot_f, initial=0.0, op0=ALU.mult, op1=ALU.add)
            dve.drain()
            dve.tensor_tensor(start_e[:], running[:, :, 0], totals[:, :, 0], ALU.subtract)
            dve.drain()
            dve.tensor_tensor(count_e[:], running[:, :, T - 1], start_e[:], ALU.subtract)
            dve.drain()
            dve.tensor_tensor(run_f, run_f, tot_f, ALU.subtract)
            dve.tensor_tensor(tiles_cmp, count_e[:, :, None].to_broadcast([P, E, T]),
                              tile_starts[:, None, :].to_broadcast([P, E, T]), ALU.is_gt)
            dve.drain()
            dve.tensor_reduce(tiles_e[:], tiles_cmp, AX.X, ALU.add)
            dve.drain()
            dve.tensor_tensor_scan(out=tiles_end[:], data0=ones[:, 0:E], data1=tiles_e[:], initial=0.0,
                                   op0=ALU.mult, op1=ALU.add)
            dve.drain()
            dve.tensor_tensor(base_e[:], tiles_end[:], tiles_e[:], ALU.subtract)
            dve.tensor_tensor(exp_cmp, tiles_end[0:1, None, :].to_broadcast([1, TILES, E]),
                              iota_j[0:1, :, None].to_broadcast([1, TILES, E]), ALU.is_le)
            dve.drain()
            dve.tensor_reduce(exp_f[:], exp_cmp, AX.X, ALU.add)
            dve.scalar_tensor_tensor(base_e[:], base_e[:], float(P), start_e[:], ALU.mult, ALU.subtract)
            dve.drain()
            dve.tensor_scalar(exp_i[:], exp_f[:], float(E - 1), None, ALU.min)
            dve.tensor_tensor(place, running.rearrange("p e i -> p i e"),
                              base_e[:, None, :].to_broadcast([P, T, E]), ALU.add)
            dve.drain().then_inc(route_ok, 1)
            dve.tensor_tensor(place, place, ps[:, 4, 0:T * E].rearrange("p (i e) -> p i e", i=T), ALU.add)
            dve.drain()
            for k in range(PICKS):
                dve.tensor_tensor(hot_w[:, :, k, :], hot[:, :, k, :], place, ALU.mult)
            dve.drain()
            dve.tensor_reduce(pos[:], hot_wg, AX.X, ALU.add)
            dve.drain()
            dve.tensor_copy(pos_i[:], pos[:])
            dve.drain()
            dve.tensor_scalar(pos_q[:], pos_i[:], P - 1, None, ALU.bitwise_and)
            dve.tensor_scalar(pos_j[:], pos_i[:], P.bit_length() - 1, None, ALU.logical_shift_right)
            dve.drain()
            dve.tensor_copy(pos_qf[:], pos_q[:])
            dve.tensor_copy(pos_jf[:], pos_j[:])
            dve.drain()
            dve.tensor_tensor(slot_hot, iota_q[:, None, :].to_broadcast([P, GROUPS, P]),
                              pos_qf[:, :, None].to_broadcast([P, GROUPS, P]), ALU.is_equal)
            dve.tensor_tensor(tile_hot[:, :, 0, :], iota_j[:, None, :].to_broadcast([P, GROUPS, TILES]),
                              pos_jf[:, :, None].to_broadcast([P, GROUPS, TILES]), ALU.is_equal)
            dve.drain()
            for k in range(PICKS):
                dve.tensor_tensor(tile_hot[:, k:GROUPS:PICKS, 1, :], tile_hot[:, k:GROUPS:PICKS, 0, :],
                                  token_id[:, :, None].to_broadcast([P, T, TILES]), ALU.mult)
            dve.tensor_tensor(tile_hot[:, :, 2, :], tile_hot[:, :, 0, :],
                              w_g[:, :, None].to_broadcast([P, GROUPS, TILES]), ALU.mult)
            dve.drain().then_inc(hot_ok, 1)
            dve.wait_ge(table_ps, 1)
            dve.tensor_copy(table, ps[:, 7, 0:3 * TILES].rearrange("p (v j) -> p v j", v=3))
            dve.drain()
            dve.tensor_copy(src_idx[:, 0:TILES], table[:, 1, :])
            dve.tensor_copy(w_slot[:], table[:, 2, :])
            dve.tensor_scalar(table[:, 0, :], table[:, 0, :], -1.0, 1.0, ALU.mult, ALU.add)
            dve.drain()
            dve.scalar_tensor_tensor(dst_idx[:], table[:, 0, :], pad_row[:, 0:1], table[:, 1, :], ALU.mult, ALU.add)
            dve.drain().then_inc(slots_ok, 1)

            dve.wait_ge(b2_in_s, 16)

            def rows(j, u):
                e = dve.value_load(exp_i[0:1, bass.ds(j, 1)], min_val=0, max_val=E - 1)
                dve.wait_ge(xgT_ps, j + 1)
                dve.tensor_copy(xgT[u], ps[:, u, :]).then_inc(xgT_sb, 1)
                return e

            def hidden(j, u):
                dve.wait_ge(hid_ps, j + 1)
                dve.tensor_copy(hid[u], ps[:, 2 + u, :]).then_inc(hid_sb, 1)

            def result(j, u):
                e = dve.value_load(exp_i[0:1, bass.ds(j, 1)], min_val=0, max_val=E - 1)
                dve.wait_ge(y_ps, j + 1)
                dve.tensor_tensor(yb[u], ps[:, 6 + u, :], b2_bc[:, bass.ds(e, 1), :].rearrange("p a n -> p (a n)"), ALU.add)
                dve.drain().then_inc(y_sb, 1)
                return e

            def weigh(j, u):
                dve.tensor_scalar(ys[u], yb[u], w_slot[:, bass.ds(j, 1)], None, ALU.mult).then_inc(ys_ready, 1)

            def transposed(j, u):
                dve.wait_ge(xgT_ps, j + 1)
                dve.tensor_copy(xgT[u], ps[:, u, :]).then_inc(xgT_sb, 1)

            transposed(0, 0)
            hidden(0, 0)
            with dve.Fori(0, (TILES - 1) // 2) as jj:
                for u in range(2):
                    j = jj * 2 + u
                    transposed(j + 1, 1 - u)
                    hidden(j + 1, 1 - u)
                    result(j, u)
                    dve.wait_ge(rows_added, j + 1)
                    weigh(j, u)
            result(TILES - 1, 0)
            dve.wait_ge(rows_added, TILES)
            weigh(TILES - 1, 0)

        @block.tensor
        def _(pe):
            pe.wait_ge(qk_in, 32)
            pe.wait_ge(consts, 2)
            pe.wait_ge(b1_in_s, 16)
            pe.transpose(ps[:, 3, 0:C], wq, ident[:])
            pe.transpose(ps[:, 3, C:2 * C], wk, ident[:])
            pe.transpose(ps[:, 3, 2 * C:2 * C + E * IB], b1_rows, ident[0:E * IB, 0:E * IB]).then_inc(wT_ps, 1)
            pe.wait_ge(wT_sb, 1)
            with pe.Fori(0, 2) as h:
                for u in range(2):
                    b = h * 2 + u
                    pe.wait_ge(ctx_in_s[u], 16 * h + 16)
                    pe.wait_ge(sim_sb, b * BT + BT)
                    for t in range(BT):
                        mm = pe.transpose(ps[:, 4 * u, t * P:(t + 1) * P], ctx_b[u][:, t * C:(t + 1) * C], ident[:])
                    mm.then_inc(ctxT_ps, 1)
                    pe.wait_ge(ctxT_sb, b + 1)
                    pe.matmul(ps[:, 4 * u + 1, :], wqT, ctxT[u], start=True, stop=True).then_inc(q_ps, 1)
                    pe.matmul(ps[:, 4 * u + 2, :], wkT, ctxT[u], start=True, stop=True).then_inc(k_ps, 1)
                    pe.wait_ge(q_sb, b + 1)
                    pe.wait_ge(k_sb, b + 1)
                    for t in range(BT):
                        pe.matmul(ps[:, 4 * u + t, :], qT[u][:, t * P:(t + 1) * P], kT[u], start=True,
                                  stop=True).then_inc(sim_ps, 1)
            pe.wait_ge(bad_sb, 1)
            pe.wait_ge(sim_sb, 2 * BT + T)
            pe.matmul(ps[0:1, 7, 0:1], bad[:], ones[:, 0:1], start=True, stop=True).then_inc(bad_ps, 1)
            pe.wait_ge(const_in, 16)
            pe.wait_ge(coef_ok, 1)
            with pe.Fori(0, 2) as h:
                for u in range(2):
                    b = h * 2 + u
                    pe.wait_ge(a_done, b * BT + BT)
                    for t in range(BT):
                        pe.wait_ge(xa_done, b * BT + t + 1)
                        pe.wait_ge(x1_sb, b * BT + t + 1)
                        pe.matmul(ps[:, t, :], ident[:], xb[:, u, t, :], start=True, stop=False)
                        pe.matmul(ps[:, t, :], ident_a[:], ab[:, u, t, :], start=False, stop=False)
                        for q in range(BT):
                            mm = pe.matmul(ps[:, t, q * P:(q + 1) * P], ab[:, u, q, t * P:(t + 1) * P], ident_a[:],
                                           start=False, stop=(q == BT - 1))
                        mm.then_inc(x1_ps, 1)
                    for t in range(BT):
                        pe.wait_ge(xn_done, b * BT + t + 1)
                        if t >= 2:
                            pe.wait_ge(xnT_sb, b * BT + t - 1)
                        for k in range(KB):
                            mm = pe.transpose(ps[:, 4 + t % 2, k * P:(k + 1) * P], xnb[:, t, k * P:(k + 1) * P], ident[:])
                        mm.then_inc(xnT_ps, 1)
                        if t == 0:
                            pe.wait_ge(log_sb, b + 1)
                        pe.wait_ge(xnT_sb, b * BT + t + 1)
                        for k in range(KB):
                            mm = pe.matmul(ps[:, 6, t * E:(t + 1) * E], xnT[:, t % 2, k * P:(k + 1) * P], gate_w[:, k, :],
                                           start=(k == 0), stop=(k == KB - 1))
                        if t == BT - 1:
                            mm.then_inc(log_ps, 1)
            pe.wait_ge(member_ok, 1)
            pe.matmul(ps[:, 4, 0:T * E], before[:], member[:], start=True, stop=True)
            pe.matmul(ps[:, 5, 0:T * E], ones_b[:], member[:], start=True, stop=True).then_inc(rank_ps, 1)
            pe.wait_ge(hot_ok, 1)
            tile_hot_g = tile_hot.rearrange("p g v j -> p g (v j)")
            for g in range(GROUPS):
                mm = pe.matmul(ps[:, 7, 0:3 * TILES], slot_hot[:, g, :], tile_hot_g[:, g, :], start=(g == 0),
                               stop=(g == GROUPS - 1))
            mm.then_inc(table_ps, 1)

            pe.wait_ge(fc1_in, 16 * E)
            pe.wait_ge(fc2_in, 16 * E)
            pe.wait_ge(route_ok, 1)
            pe.wait_ge(slots_ok, 1)

            def expert(j):
                return pe.value_load(exp_i[0:1, bass.ds(j, 1)], min_val=0, max_val=E - 1)

            def w_block(e, m, k):
                return weights[:, bass.ds(e, 1), m, k, :].rearrange("p a n -> p (a n)")

            def layer1(j, u, arrivals):
                pe.wait_ge(gathered[u], arrivals)
                for k in range(KB):
                    mm = pe.transpose(ps[:, u, k * P:(k + 1) * P], xg[u][:, k * P:(k + 1) * P], ident[:])
                mm.then_inc(xgT_ps, 1)
                e = expert(j)
                pe.wait_ge(xgT_sb, j + 1)
                for k in range(KB):
                    mm = pe.matmul(ps[:, 2 + u, :], xgT[u][:, k * P:(k + 1) * P], w_block(e, 0, k), start=(k == 0),
                                   stop=(k == KB - 1))
                mm.then_inc(hid_ps, 1)

            def turn_hidden(j, u):
                pe.wait_ge(hid_sb, j + 1)
                for i in range(IB):
                    mm = pe.transpose(ps[:, 4 + u, i * P:(i + 1) * P], hid[u][:, i * P:(i + 1) * P], ident[:])
                mm.then_inc(hidT_ps, 1)

            def layer2(j, u):
                e = expert(j)
                pe.wait_ge(gelu_sb, j + 1)
                pe.wait_ge(y_sb, j + 1)
                for i in range(IB):
                    mm = pe.matmul(ps[:, 6 + u, :], act_t[u][:, i * P:(i + 1) * P], w_block(e, 1, i), start=(i == 0),
                                   stop=(i == IB - 1))
                mm.then_inc(y_ps, 1)

            layer1(0, 0, 16)
            with pe.Fori(0, (TILES - 1) // 2) as jj:
                for u in range(2):
                    j = jj * 2 + u
                    turn_hidden(j, u)
                    layer1(j + 1, 1 - u, 16 * jj + (16 if u == 0 else 32))
                    layer2(j, u)
            turn_hidden(TILES - 1, 0)
            layer2(TILES - 1, 0)


_INS = ["x", "ctx_512", "g_xattn", "g_ffn", "L0_xattn_Wq", "L0_xattn_Wk", "L0_xattn_gamma_raw", "L0_ffn_gate_w",
        "L0_ffn_fc1_w", "L0_ffn_fc1_b", "L0_ffn_fc2_w", "L0_ffn_fc2_b", "L0_ffn_alpha"]


def kernel(**inputs):
    import concourse.bacc as bacc
    from concourse.bass_utils import run_bass_kernel_spmd as run

    nc = bacc.Bacc("TRN2", target_bir_lowering=False, num_devices=1, dynamic_dma_scratch_size=8192)
    arrays, args = {}, []
    for name in _INS:
        a = np.ascontiguousarray(inputs[name])
        if name in ("x", "ctx_512"):
            a = a.reshape(TOKENS, -1)
        if a.ndim == 0:
            a = a.reshape(1)
        arrays[f"in_{name}"] = a
        args.append(nc.dram_tensor(f"in_{name}", a.shape, mybir.dt.from_np(a.dtype), kind="ExternalInput").ap())
    xn_rows = nc.dram_tensor("xn_rows", (TOKENS, D), F32, kind="Internal").ap()
    out_rows = nc.dram_tensor("out_rows", (TOKENS + P, D), F32, kind="ExternalOutput").ap()
    build(nc, *args, xn_rows, out_rows)
    r = run(nc, [arrays], core_ids=[0])
    return r.results[0]["out_rows"][:TOKENS].reshape(BATCH, SEQ, D)
```

```python
from contextlib import ExitStack

import concourse.bass as bass
import numpy as np
from concourse import mybir

F32 = mybir.dt.float32
BF16 = mybir.dt.bfloat16
I32 = mybir.dt.int32
U32 = mybir.dt.uint32
ALU = mybir.AluOpType
ACT = mybir.ActivationFunctionType
AX = mybir.AxisListType

P = 128
BATCH, SEQ, D = 4, 512, 512
C = 128
HEADS = 4
E = 8
PICKS = 2
INTER = 512
TOKENS = BATCH * SEQ
T = TOKENS // P
BT = SEQ // P
KB = D // P
IB = INTER // P
TOPK = int(SEQ * 0.3)
GROUPS = T * PICKS
TILES = (TOKENS * PICKS + E * (P - 1)) // P
LN_EPS = 1e-5
SIM_SCALE = float(np.float32(1.0) / (np.sqrt(np.float32(C // HEADS)) * np.float32(HEADS)))

ROUNDS = 6
T_DVE = 9
WINDOW = 8
BELOW = SEQ - TOPK
AIM = BELOW + WINDOW / 2
START_SIGMAS = 0.55
DENSITY = 0.35
BRACKET_LOW, BRACKET_HIGH = 3.0, 3.5
AHEAD = 4
BIG = 1e30
LOWEST = -3e38


def build(nc, x, ctx_in, g_x, g_f, wq_in, wk_in, gam_in, gate_in, fc1, b1_in, fc2, b2_in, alpha_in, xn_rows, out_rows):
    es = ExitStack()
    with es:
        def sb(name, shape, dt=F32):
            return es.enter_context(nc.sbuf_tensor(name, shape, dt))

        def sem(name):
            return es.enter_context(nc.semaphore(name))

        weights = sb("weights", [P, E, 2, KB, INTER])
        sim = sb("sim", [P, T, SEQ])
        xb = sb("xb", [P, 2, BT, D])
        ab = sb("ab", [P, 2, BT, SEQ])
        xnb = sb("xnb", [P, BT, D])
        xnT = sb("xnT", [P, 2, D])
        ab_flat = ab[:].rearrange("p u t n -> p (u t n)")
        sim_flat = sim[:].rearrange("p t n -> p (t n)")
        ctx_b = [ab_flat[:, u * 2048:u * 2048 + 512] for u in range(2)]
        ctxT = [ab_flat[:, u * 2048 + 512:u * 2048 + 1024] for u in range(2)]
        qT = [ab_flat[:, u * 2048 + 1024:u * 2048 + 1536] for u in range(2)]
        kT = [ab_flat[:, u * 2048 + 1536:u * 2048 + 2048] for u in range(2)]
        slot_hot = sim_flat[:, 0:GROUPS * P].rearrange("p (g q) -> p g q", g=GROUPS)
        tile_hot = ab_flat[:, 0:GROUPS * 3 * TILES].rearrange("p (g v j) -> p g v j", g=GROUPS, v=3)
        b2_bc = xb[:].rearrange("p u t n -> p (u t n)").rearrange("p (e n) -> p e n", e=E)

        def ring(at, n=2):
            return [sim_flat[:, (at + u) * 512:(at + u + 1) * 512] for u in range(n)]

        xg, xgT, hid, act_t, yb, ys = ring(0), ring(2), ring(4), ring(6), ring(8), ring(10)

        xnb_flat = xnb[:].rearrange("p t n -> p (t n)")
        wq, wk, wqT, wkT = (xnb_flat[:, n * C:(n + 1) * C] for n in range(4))
        b1_rows = xnb_flat[0:E * IB, 512:640]
        junk = ab_flat.bitcast(BF16).rearrange("p (i n) -> p i n", i=T)
        hot = sim_flat[:, 6144:6400].rearrange("p (i k e) -> p i k e", k=PICKS, e=E)
        hot_w = sim_flat[:, 6400:6656].rearrange("p (i k e) -> p i k e", k=PICKS, e=E)
        totals, running, tiles_cmp = (sim_flat[:, at:at + T * E].rearrange("p (e i) -> p e i", e=E) for at in (6656, 6784, 6912))
        place = sim_flat[:, 7040:7168].rearrange("p (i e) -> p i e", e=E)

        exp_cmp = sim_flat[0:1, 7168:7168 + TILES * E].rearrange("p (j e) -> p j e", e=E)
        table = sim_flat[:, 7488:7488 + 3 * TILES].rearrange("p (v j) -> p v j", v=3)
        top, pick = (ab_flat[:, at:at + T * WINDOW].rearrange("p (i w) -> p i w", w=WINDOW) for at in (0, 128))
        pad_zero = xnb_flat[:, 1536:1536 + D]
        penal = [ab_flat[:, n * SEQ:(n + 1) * SEQ] for n in range(1, 8)]

        ident = sb("ident", [P, P])
        ident_a = sb("ident_a", [P, P])
        before = sb("before", [P, P], BF16)
        ones_b = sb("ones_b", [P, P], BF16)
        ones = sb("ones", [P, T * E])
        gate_w = sb("gate_w", [P, KB, E])
        b1T = sb("b1T", [P, E * IB])
        raw = sb("raw", [P, 3])
        alpha_bc = sb("alpha_bc", [P, E])
        coef = sb("coef", [P, 8])
        iota_e = sb("iota_e", [P, E])
        iota_q = sb("iota_q", [P, P])
        iota_j = sb("iota_j", [P, TILES])
        tile_starts = sb("tile_starts", [P, T])
        token_id = sb("token_id", [P, T])
        pad_row = sb("pad_row", [P, 1])

        stats = sb("stats", [P, T, 6])
        mv = sb("mv", [P, T, 2])
        dev = sb("dev", [P, T])
        t_now = sb("t_now", [P, T])
        hi_big = sb("hi_big", [P, T])
        cnt = sb("cnt", [P, T])
        lo = sb("lo", [P, T])
        hi = sb("hi", [P, T])
        n_lo = sb("n_lo", [P, T])
        n_hi = sb("n_hi", [P, T])
        most, aim, proof, unit = (sb(n, [P, T]) for n in ("most", "aim", "proof", "unit"))
        half = sb("half", [P, T])
        neg_half = sb("neg_half", [P, T])
        var_s = sb("var_s", [P, T])
        var_x = sb("var_x", [P, T])
        width = sb("width", [P, T])
        over = sb("over", [P, T], I32)
        under = sb("under", [P, T], I32)
        tmp0 = sb("tmp0", [P, T])
        tmp1 = sb("tmp1", [P, T])
        thr = sb("thr", [P, T])
        bad = sb("bad", [P, 1])
        bad_i = sb("bad_i", [1, 1], I32)
        work = sb("work", [P, 8])

        statx = sb("statx", [P, T, 6])
        mvx = sb("mvx", [P, T, 2])
        rstd_x = sb("rstd_x", [P, T])
        xa_scale = sb("xa_scale", [P, T])
        xa_bias = sb("xa_bias", [P, T])
        stat1 = sb("stat1", [P, BT, 6])
        mv1 = sb("mv1", [P, 2, BT, 2])
        var1 = sb("var1", [P, BT])
        xn_scale = sb("xn_scale", [P, 2, BT])
        xn_bias = sb("xn_bias", [P, 2, BT])

        logits = sb("logits", [P, T, E])
        best = sb("best", [P, T, E])
        best_i = sb("best_i", [P, T, E], U32)
        idx_f = sb("idx_f", [P, T, PICKS])
        member = sb("member", [P, T * E], BF16)
        gap = sb("gap", [P, T])
        score = sb("score", [P, T, PICKS])
        w_tok = sb("w_tok", [P, T, PICKS])
        count_e = sb("count_e", [P, E])
        start_e = sb("start_e", [P, E])
        tiles_e = sb("tiles_e", [P, E])
        tiles_end = sb("tiles_end", [P, E])
        base_e = sb("base_e", [P, E])
        pos = sb("pos", [P, GROUPS])
        pos_i = sb("pos_i", [P, GROUPS], I32)
        pos_q = sb("pos_q", [P, GROUPS], I32)
        pos_j = sb("pos_j", [P, GROUPS], I32)
        pos_qf = sb("pos_qf", [P, GROUPS])
        pos_jf = sb("pos_jf", [P, GROUPS])
        exp_f = sb("exp_f", [1, TILES])
        exp_i = sb("exp_i", [1, TILES], I32)
        w_slot = sb("w_slot", [P, TILES])
        src_idx = sb("src_idx", [P, TILES + 1], U32)
        dst_idx = sb("dst_idx", [P, TILES], U32)

        src_now = sb("src_now", [P, 2], U32)
        dst_now = sb("dst_now", [P, 2], U32)

        ps = es.enter_context(nc.psum_tensor("ps", [P, 8, 512], F32))

        const_in, qk_in, b1_in_s, scal_in = sem("const_in"), sem("qk_in"), sem("b1_in_s"), sem("scal_in")
        ctx_in_s = [sem("ctx_in0"), sem("ctx_in1")]
        x_in = [sem("x_in0"), sem("x_in1")]
        fc1_in, fc2_in, b2_in_s = sem("fc1_in"), sem("fc2_in"), sem("b2_in_s")
        consts = sem("consts")
        wT_ps, wT_sb = sem("wT_ps"), sem("wT_sb")
        coef_ok = sem("coef_ok")
        ctxT_ps, ctxT_sb, q_ps, k_ps, qk_sb = (sem(n) for n in ("ctxT_ps", "ctxT_sb", "q_ps", "k_ps", "qk_sb"))
        sim_ps, sim_sb = sem("sim_ps"), sem("sim_sb")
        trial, counted, pen_done, pen_used = sem("trial"), sem("counted"), sem("pen_done"), sem("pen_used")
        bad_sb, bad_ps, thr_ok = sem("bad_sb"), sem("bad_ps"), sem("thr_ok")
        act_coef, sig_done, a_done, xa_done = sem("act_coef"), sem("sig_done"), sem("a_done"), sem("xa_done")
        parked_read, var_ok, dev_ok, rstd_ok = sem("parked_read"), sem("var_ok"), sem("dev_ok"), sem("rstd_ok")
        x1_var, x1_rstd, pen_less = sem("x1_var"), sem("x1_rstd"), sem("pen_less")
        x_parked = [sem("x_parked0"), sem("x_parked1")]
        x1_ps, x1_sb, xn_coef, xn_done = (sem(n) for n in ("x1_ps", "x1_sb", "xn_coef", "xn_done"))
        xnT_ps, xnT_sb, log_ps, log_sb = sem("xnT_ps"), sem("xnT_sb"), sem("log_ps"), sem("log_sb")
        xn_out, x1_out, pad_out = sem("xn_out"), sem("x1_out"), sem("pad_out")
        gap_ok, score_ok, member_ok, rank_ps, hot_ok, table_ps, route_ok, slots_ok = (
            sem(n) for n in ("gap_ok", "score_ok", "member_ok", "rank_ps", "hot_ok", "table_ps", "route_ok", "slots_ok"))
        src_set, dst_set, pool_turn, rows_added = sem("src_set"), sem("dst_set"), sem("pool_turn"), sem("rows_added")
        gathered = [sem("gathered0"), sem("gathered1")]
        scattered = [sem("scattered0"), sem("scattered1")]
        xgT_ps, xgT_sb, hid_ps, hid_sb, hidT_ps, gelu_sb, y_ps, y_sb, ys_ready = (
            sem(n) for n in ("xgT_ps", "xgT_sb", "hid_ps", "hid_sb", "hidT_ps", "gelu_sb", "y_ps", "y_sb", "ys_ready"))

        ctx_v = ctx_in.rearrange("(b t p) c -> b p t c", t=BT, p=P)
        x_v = x.rearrange("(b t p) n -> b p t n", t=BT, p=P)
        xn_v = xn_rows.rearrange("(b t p) n -> b p t n", t=BT, p=P)
        out_v = out_rows[0:TOKENS, :].rearrange("(b t p) n -> b p t n", t=BT, p=P)

        def bc_row(v, n):
            return v.rearrange("(a b) -> a b", a=1).to_broadcast([P, n])

        block = es.enter_context(nc.Block())

        @block.sync
        def _(sp):
            sp.dma_start(wq, wq_in).then_inc(qk_in, 16)
            sp.dma_start(wk, wk_in).then_inc(qk_in, 16)
            for u in range(2):
                sp.dma_start(ctx_b[u].rearrange("p (t c) -> p t c", t=BT), ctx_v[u]).then_inc(ctx_in_s[u], 16)
            for n, g in enumerate((g_x, g_f, gam_in)):
                sp.dma_start(raw[:, n:n + 1], bc_row(g, 1)).then_inc(scal_in, 16)
            sp.dma_start(alpha_bc[:], bc_row(alpha_in, E)).then_inc(scal_in, 16)
            sp.dma_start(b1_rows, b1_in.rearrange("e (i p) -> (e i) p", p=P)).then_inc(b1_in_s, 16)
            sp.dma_start(gate_w[:], gate_in.rearrange("(k p) e -> p k e", p=P)).then_inc(const_in, 16)
            for u in range(2):
                sp.dma_start(sim[:, (2 + u) * BT:(3 + u) * BT], x_v[2 + u]).then_inc(x_parked[u], 16)
            for u in range(2):
                sp.wait_ge(ctxT_ps, u + 1)
                sp.dma_start(ctx_b[u].rearrange("p (t c) -> p t c", t=BT), ctx_v[2 + u]).then_inc(ctx_in_s[u], 16)
            for u in range(2):
                sp.dma_start(xb[:, u], x_v[u]).then_inc(x_in[u], 16)
            for e in range(E):
                for m, (fc, s) in enumerate(((fc1, fc1_in), (fc2, fc2_in))):
                    sp.dma_start(weights[:, e, m], fc[e].rearrange("(k p) n -> p k n", p=P)).then_inc(s, 16)
            sp.wait_ge(consts, 1)
            sp.dma_start(out_rows[TOKENS:TOKENS + P, :], pad_zero).then_inc(pad_out, 16)
            for b in range(BATCH):
                u = b % 2
                sp.wait_ge(x1_sb, BT + BT * (b + 1))
                sp.dma_start(out_v[b], xb[:, u]).then_inc(x1_out, 16)
                sp.wait_ge(xn_done, BT * (b + 1))
                sp.dma_start(xn_v[b], xnb[:]).then_inc(xn_out, 16)
                if b + 2 < BATCH:
                    sp.wait_ge(x1_out, 16 * (b + 1))
                    sp.dma_start(xb[:, u], x_v[b + 2]).then_inc(x_in[u], 16)
            sp.wait_ge(x1_out, 16 * BATCH)
            sp.dma_start(b2_bc, b2_in.rearrange("(a e) n -> a e n", a=1).to_broadcast([P, E, D])).then_inc(b2_in_s, 16)

        @block.gpsimd
        def _(pool):
            pool.memset(pad_zero, 0.0).then_inc(consts, 1)
            pool.memset(ident[:], 0.0)
            pool.memset(ones_b[:], 1.0)
            pool.memset(ones[:], 1.0)
            pool.drain()
            pool.affine_select(out=ident[:], in_=ident[:], compare_op=ALU.not_equal, fill=1.0, base=0,
                               pattern=[[-1, P]], channel_multiplier=1).then_inc(consts, 1)
            pool.affine_select(out=before[:], in_=ones_b[:], compare_op=ALU.is_gt, fill=0.0, base=0,
                               pattern=[[1, P]], channel_multiplier=-1)
            for buf, pattern, base, by in (
                (iota_e[:], [[1, E]], 0, 0), (iota_q[:], [[1, P]], 0, 0), (iota_j[:], [[1, TILES]], 0, 0),
                (tile_starts[:], [[P, T]], 0, 0), (token_id[:], [[P, T]], 0, 1), (pad_row[:], [[1, 1]], TOKENS, 1),
            ):
                pool.iota(buf, pattern, base=base, channel_multiplier=by, allow_small_or_imprecise_dtypes=True)
            pool.memset(src_idx[:], 0)
            for cols, n_of, step in ((slice(0, T_DVE), lambda n: float(n), 1.0),
                                     (slice(T_DVE, T), lambda n: float(2 * n - SEQ), 0.5)):
                pool.memset(most[:, cols], n_of(BELOW))
                pool.memset(aim[:, cols], n_of(AIM))
                pool.memset(n_lo[:, cols], n_of(0))
                pool.memset(n_hi[:, cols], n_of(SEQ))
                pool.memset(unit[:, cols], step / (SEQ * DENSITY))
            pool.memset(proof[:, 0:T_DVE], float(BELOW))
            pool.memset(proof[:, T_DVE:T], float(2 * BELOW - SEQ + 1))
            pool.memset(half[:], 0.5)
            pool.memset(neg_half[:], -0.5)
            pool.drain().then_inc(consts, 1)

            pool.wait_ge(var_ok, 1)
            pool.tensor_tensor(dev[:], var_s[:], half[:], ALU.pow)
            pool.drain().then_inc(dev_ok, 1)
            pool.tensor_tensor(rstd_x[:], var_x[:], neg_half[:], ALU.pow)
            pool.drain().then_inc(rstd_ok, 1)
            for i in range(1, T, 2):
                pool.wait_ge(pen_done, i + 1)
                pool.tensor_tensor(penal[i % 7], sim[:, i, :], penal[i % 7], ALU.subtract).then_inc(pen_less, 1)
            with pool.Fori(0, 2) as h:
                for u in range(2):
                    pool.wait_ge(x1_var, h * 2 + u + 1)
                    pool.sem_inc(pool_turn, 1)
                    pool.tensor_scalar(var1[:], mv1[:, u, :, 1], LN_EPS, None, ALU.add)
                    pool.drain()
                    pool.tensor_tensor(xn_scale[:, u, :], var1[:], neg_half[:, 0:BT], ALU.pow)
                    pool.drain().then_inc(x1_rstd, 1)

            pool.wait_ge(xn_out, 16 * BATCH + 16)
            pool.wait_ge(x1_out, 16 * BATCH)
            pool.wait_ge(pad_out, 16)
            pool.wait_ge(slots_ok, 1)

            last_token, last_row = pool.to_reg(TOKENS - 1), pool.to_reg(TOKENS + P - 1)

            def gather(j, u):
                pool.tensor_copy(src_now[:, u:u + 1], src_idx[:, bass.ds(j, 1)]).then_inc(src_set, 1)
                pool.wait_ge(src_set, j + 1)
                pool.sem_inc(pool_turn, 1)
                pool.indirect_dma_start(
                    out=xg[u], out_offset=None, in_=xn_rows,
                    in_offset=bass.IndirectOffsetOnAxis(ap=src_now[:, u:u + 1], axis=0),
                    bounds_check=last_token).then_inc(gathered[u], 16)

            def scatter(j, u):
                pool.tensor_copy(dst_now[:, u:u + 1], dst_idx[:, bass.ds(j, 1)]).then_inc(dst_set, 1)
                pool.wait_ge(dst_set, j + 1)
                pool.wait_ge(ys_ready, j + 1)
                pool.sem_inc(pool_turn, 1)
                pool.indirect_dma_start(
                    out=out_rows, out_offset=bass.IndirectOffsetOnAxis(ap=dst_now[:, u:u + 1], axis=0),
                    in_=ys[u], in_offset=None, bounds_check=last_row,
                    compute_op=ALU.add).then_inc(scattered[u], 16)

            def added(u, scatters):
                pool.wait_ge(scattered[u], scatters)
                pool.sem_inc(rows_added, 1)

            gather(0, 0)
            gather(1, 1)
            for j in range(2, AHEAD):
                pool.wait_ge(xgT_ps, j - 1)
                gather(j, j % 2)
            with pool.Fori(0, (TILES - AHEAD) // 2) as jj:
                for u in range(2):
                    j = jj * 2 + u
                    scatter(j, u)
                    pool.wait_ge(xgT_ps, j + AHEAD - 1)
                    gather(j + AHEAD, u)
                    added(u, 16 * jj + 16)
            for j in range((TILES - AHEAD) // 2 * 2, TILES):
                scatter(j, j % 2)
                if j + AHEAD < TILES:
                    pool.wait_ge(xgT_ps, j + AHEAD - 1)
                    gather(j + AHEAD, j % 2)
                added(j % 2, 16 * (j // 2 + 1))

        @block.scalar
        def _(act):
            act.sem_inc(sim_sb, 2 * BT)
            act.sem_inc(x1_sb, BT)
            act.wait_ge(scal_in, 64)
            act.activation(coef[:, 0:2], raw[:, 0:2], ACT.Tanh)
            act.activation(coef[:, 2:3], raw[:, 2:3], ACT.Sigmoid).then_inc(act_coef, 1)
            act.wait_ge(qk_in, 32)
            act.wait_ge(wT_ps, 1)
            act.copy(wqT, ps[:, 3, 0:C])
            act.copy(wkT, ps[:, 3, C:2 * C])
            act.copy(b1T[:], ps[:, 3, 2 * C:2 * C + E * IB])
            act.drain().then_inc(wT_sb, 1)
            with act.Fori(0, 2) as h:
                for u in range(2):
                    b = h * 2 + u
                    act.wait_ge(ctxT_ps, b + 1)
                    act.copy(ctxT[u], ps[:, 4 * u, :]).then_inc(ctxT_sb, 1)
                    act.wait_ge(q_ps, b + 1)
                    act.copy(qT[u], ps[:, 4 * u + 1, :])
                    act.wait_ge(k_ps, b + 1)
                    act.copy(kT[u], ps[:, 4 * u + 2, :]).then_inc(qk_sb, 1)
                    act.wait_ge(parked_read, h + 1)
                    for t in range(BT):
                        act.wait_ge(sim_ps, b * BT + t + 1)
                        act.activation(sim[:, bass.ds(b * BT + t, 1), :].rearrange("p a n -> p (a n)"),
                                       ps[:, 4 * u + t, :], ACT.Copy, scale=SIM_SCALE).then_inc(sim_sb, 1)
            act.drain()

            def sign_sums():
                for i in range(T_DVE, T):
                    last = act.activation(junk[:, i, :], sim[:, i, :], ACT.Sign, bias=t_now[:, i:i + 1], scale=-1.0,
                                          accum_out=cnt[:, i:i + 1])
                last.then_inc(counted, 1)
                act.drain()

            with act.Fori(0, ROUNDS) as r:
                act.wait_ge(trial, r + 1)
                sign_sums()
            act.wait_ge(trial, ROUNDS + 1)
            for i in range(T):
                if i >= 7:
                    act.wait_ge(pen_used, i - 6)
                act.activation(penal[i % 7], sim[:, i, :], ACT.Relu, bias=hi_big[:, i:i + 1],
                               scale=BIG).then_inc(pen_done, 1)
            act.wait_ge(trial, ROUNDS + 2)
            sign_sums()
            act.wait_ge(bad_sb, 1)
            act.wait_ge(pad_out, 16)
            act.wait_ge(coef_ok, 2)
            with act.Fori(0, 2) as h:
                for u in range(2):
                    b = h * 2 + u
                    act.wait_ge(x1_ps, b * BT + BT)
                    for t in range(BT):
                        act.activation(ab[:, u, t, :], sim[:, bass.ds(b * BT + t, 1), :].rearrange("p a n -> p (a n)"),
                                       ACT.Sigmoid).then_inc(sig_done, 1)
                for u in range(2):
                    b = h * 2 + u
                    act.wait_ge(x_in[u], 16 * h + 16)
                    for t in range(BT):
                        act.activation(xb[:, u, t, :], xb[:, u, t, :], ACT.Identity, scale=xa_scale[:, bass.ds(b * BT + t, 1)],
                                       bias=xa_bias[:, bass.ds(b * BT + t, 1)]).then_inc(xa_done, 1)
                for u in range(2):
                    b = h * 2 + u
                    act.wait_ge(xn_coef, b + 1)
                    act.wait_ge(xn_out, b * 16 + 16)
                    act.wait_ge(xnT_ps, b * BT + 4)
                    for t in range(BT):
                        act.activation(xnb[:, t, :], xb[:, u, t, :], ACT.Identity, scale=xn_scale[:, u, t:t + 1],
                                       bias=xn_bias[:, u, t:t + 1]).then_inc(xn_done, 1)
                    for t in range(BT):
                        act.wait_ge(xnT_ps, b * BT + t + 5)
                        act.copy(xnT[:, t % 2, :], ps[:, 4 + t % 2, :]).then_inc(xnT_sb, 1)
                    act.wait_ge(log_ps, b + 1)
                    act.copy(logits[:, bass.ds(b * BT, BT), :].rearrange("p t e -> p (t e)"),
                             ps[:, 6, 0:BT * E]).then_inc(log_sb, 1)
            act.wait_ge(gap_ok, 1)
            act.activation(score[:, :, 0], gap[:], ACT.Sigmoid)
            act.activation(score[:, :, 1], gap[:], ACT.Sigmoid, scale=-1.0).then_inc(score_ok, 1)

            act.wait_ge(route_ok, 1)

            def gelu(j, u):
                e = act.value_load(exp_i[0:1, bass.ds(j, 1)], min_val=0, max_val=E - 1)
                act.wait_ge(hidT_ps, j + 1)
                for i in range(IB):
                    last = act.activation(act_t[u][:, i * P:(i + 1) * P], ps[:, 4 + u, i * P:(i + 1) * P], ACT.Gelu,
                                          bias=b1T[:, bass.ds(e * IB + i, 1)])
                last.then_inc(gelu_sb, 1)

            with act.Fori(0, (TILES - 1) // 2) as jj:
                for u in range(2):
                    gelu(jj * 2 + u, u)
            gelu(TILES - 1, 0)

        @block.vector
        def _(dve):
            dve.wait_ge(act_coef, 1)
            dve.tensor_scalar(coef[:, 5:6], coef[:, 2:3], -1.0, 1.0, ALU.mult, ALU.add)
            dve.tensor_scalar(coef[:, 4:5], coef[:, 2:3], coef[:, 0:1], 0.5, ALU.mult, ALU.mult)
            dve.drain()
            dve.tensor_tensor(coef[:, 3:4], coef[:, 5:6], coef[:, 0:1], ALU.mult)
            dve.wait_ge(consts, 3)
            dve.tensor_scalar(ident_a[:], ident[:], coef[:, 4:5], None, ALU.mult)
            dve.drain().then_inc(coef_ok, 1)
            dve.sem_inc(x1_ps, 2 * BT)
            dve.sem_inc(xn_out, 16)
            dve.sem_inc(xnT_ps, BT)
            dve.sem_inc(log_sb, 1)
            dve.sem_inc(y_sb, 2)
            dve.sem_inc(rows_added, 2)
            dve.sem_inc(parked_read, 1)

            for u in range(2):
                dve.wait_ge(x_parked[u], 16)
                for t in range(BT):
                    i = (2 + u) * BT + t
                    last = dve.bn_stats(statx[:, i, :], sim[:, i, :])
            last.then_inc(parked_read, 1)
            for u in range(2):
                dve.wait_ge(x_in[u], 16)
                for t in range(BT):
                    dve.bn_stats(statx[:, u * BT + t, :], xb[:, u, t, :])
            with dve.Fori(0, T) as i:
                dve.wait_ge(sim_sb, 2 * BT + i + 1)
                dve.bn_stats(stats[:, bass.ds(i, 1), :].rearrange("p a n -> p (a n)"),
                             sim[:, bass.ds(i, 1), :].rearrange("p a n -> p (a n)"))
            dve.drain()
            for i in range(T):
                dve.bn_aggr(mv[:, i, :], stats[:, i, :])
                dve.bn_aggr(mvx[:, i, :], statx[:, i, :])
            dve.drain()
            mean = mv[:, :, 0]
            dve.tensor_scalar(var_s[:], mv[:, :, 1], 1e-30, None, ALU.max)
            dve.tensor_scalar(var_x[:], mvx[:, :, 1], LN_EPS, None, ALU.add)
            dve.drain().then_inc(var_ok, 1)
            dve.wait_ge(dev_ok, 1)
            dve.scalar_tensor_tensor(t_now[:], dev[:], START_SIGMAS, mean, ALU.mult, ALU.add)
            dve.drain().then_inc(trial, 1)
            dve.scalar_tensor_tensor(lo[:], dev[:], -BRACKET_LOW, mean, ALU.mult, ALU.add)
            dve.scalar_tensor_tensor(hi[:], dev[:], BRACKET_HIGH, mean, ALU.mult, ALU.add)
            dve.tensor_tensor(dev[:], dev[:], unit[:], ALU.mult)

            def count(rounds):
                for i in range(T_DVE):
                    dve.tensor_scalar(junk[:, i, :], sim[:, i, :], t_now[:, i:i + 1], None, ALU.is_lt, ALU.add,
                                      accum_out=cnt[:, i:i + 1])
                dve.drain()
                dve.wait_ge(counted, rounds)

            def narrow():
                dve.tensor_tensor(over[:], cnt[:], most[:], ALU.is_le)
                dve.tensor_tensor(under[:], cnt[:], most[:], ALU.is_gt)
                dve.drain()
                dve.copy_predicated(lo[:], over[:], t_now[:])
                dve.copy_predicated(n_lo[:], over[:], cnt[:])
                dve.copy_predicated(hi[:], under[:], t_now[:])
                dve.copy_predicated(n_hi[:], under[:], cnt[:])

            count(1)
            narrow()
            dve.tensor_tensor(tmp0[:], aim[:], cnt[:], ALU.subtract)
            dve.drain()
            dve.tensor_tensor(tmp1[:], tmp0[:], dev[:], ALU.mult)
            dve.drain()
            dve.tensor_tensor(t_now[:], t_now[:], tmp1[:], ALU.add)
            dve.drain().then_inc(trial, 1)
            with dve.Fori(1, ROUNDS - 1) as r:
                count(r + 1)
                narrow()
                dve.drain()
                dve.tensor_tensor(tmp0[:], n_hi[:], n_lo[:], ALU.subtract)
                dve.tensor_tensor(tmp1[:], n_hi[:], aim[:], ALU.subtract)
                dve.tensor_tensor(width[:], lo[:], hi[:], ALU.subtract)
                dve.drain()
                dve.scalar_tensor_tensor(tmp1[:], tmp0[:], 0.05, tmp1[:], ALU.mult, ALU.max)
                dve.reciprocal(cnt[:], tmp0[:])
                dve.drain()
                dve.tensor_tensor(tmp1[:], tmp1[:], cnt[:], ALU.mult)
                dve.drain()
                dve.scalar_tensor_tensor(tmp1[:], tmp1[:], 0.95, width[:], ALU.min, ALU.mult)
                dve.drain()
                dve.tensor_tensor(t_now[:], tmp1[:], hi[:], ALU.add)
                dve.drain().then_inc(trial, 1)
            count(ROUNDS)
            narrow()
            dve.drain()
            dve.tensor_scalar(hi_big[:], hi[:], -BIG, None, ALU.mult)
            dve.drain().then_inc(trial, 1)
            dve.wait_ge(rstd_ok, 1)
            dve.tensor_scalar(tmp0[:], rstd_x[:], coef[:, 3:4], None, ALU.mult)
            dve.drain()
            dve.tensor_scalar(xa_scale[:], tmp0[:], 1.0, None, ALU.add)
            dve.scalar_tensor_tensor(xa_bias[:], tmp0[:], -1.0, mvx[:, :, 0], ALU.mult, ALU.mult)
            dve.drain().then_inc(coef_ok, 1)
            for i in range(T):
                dve.wait_ge(pen_done, i + 1)
                if i % 2 == 0:
                    dve.tensor_tensor(penal[i % 7], sim[:, i, :], penal[i % 7], ALU.subtract)
                    dve.drain()
                else:
                    dve.wait_ge(pen_less, i // 2 + 1)
                dve.max(out=top[:, i, :], in_=penal[i % 7]).then_inc(pen_used, 1)
            dve.tensor_scalar(tmp0[:, 0:T_DVE], n_hi[:, 0:T_DVE], float(TOPK - 1 - SEQ), None, ALU.add)
            dve.tensor_scalar(tmp0[:, T_DVE:T], n_hi[:, T_DVE:T], 0.5, TOPK - 1 - SEQ / 2, ALU.mult, ALU.add)
            dve.drain()
            dve.tensor_tensor(pick, iota_e[:, None, :].to_broadcast([P, T, WINDOW]),
                              tmp0[:, :, None].to_broadcast([P, T, WINDOW]), ALU.is_equal)
            dve.drain()
            dve.tensor_tensor(pick, pick, top, ALU.mult)
            dve.drain()
            dve.tensor_reduce(t_now[:], pick, AX.X, ALU.add)
            dve.drain().then_inc(trial, 1)
            dve.tensor_copy(thr[:], t_now[:])
            count(ROUNDS + 1)
            dve.tensor_tensor(tmp0[:], cnt[:], proof[:], ALU.not_equal)
            dve.drain()
            dve.tensor_reduce(bad[:], tmp0[:], AX.X, ALU.add)
            dve.drain().then_inc(bad_sb, 1)
            dve.wait_ge(bad_ps, 1)
            dve.tensor_copy(bad_i[:], ps[0:1, 7, 0:1])
            dve.drain()
            unproved = dve.value_load(bad_i[0:1, 0:1], min_val=0, max_val=TOKENS)
            with dve.If(unproved > 0):
                with dve.Fori(0, T) as i:
                    dve.tensor_copy(xnT[:, 0, :], sim[:, bass.ds(i, 1), :].rearrange("p a n -> p (a n)"))
                    dve.drain()
                    with dve.Fori(0, (TOPK - 1) // WINDOW):
                        dve.max(out=work[:], in_=xnT[:, 0, :])
                        dve.drain()
                        dve.match_replace(out=xnT[:, 0, :], in_to_replace=work[:], in_values=xnT[:, 0, :],
                                          imm_value=LOWEST)
                        dve.drain()
                    dve.max(out=work[:], in_=xnT[:, 0, :])
                    dve.drain()
                    dve.tensor_copy(thr[:, bass.ds(i, 1)], work[:, (TOPK - 1) % WINDOW:(TOPK - 1) % WINDOW + 1])
                    dve.drain()
            with dve.Else():
                dve.drain()
            dve.drain()

            def norm_coefs(b, u):
                dve.wait_ge(x1_rstd, b + 1)
                dve.scalar_tensor_tensor(xn_bias[:, u, :], xn_scale[:, u, :], -1.0, mv1[:, u, :, 0], ALU.mult, ALU.mult)
                dve.drain().then_inc(xn_coef, 1)

            with dve.Fori(0, 2) as h:
                for u in range(2):
                    b = h * 2 + u
                    for t in range(BT):
                        dve.wait_ge(sig_done, b * BT + t + 1)
                        dve.scalar_tensor_tensor(
                            ab[:, u, t, :], sim[:, bass.ds(b * BT + t, 1), :].rearrange("p a n -> p (a n)"),
                            thr[:, bass.ds(b * BT + t, 1)], ab[:, u, t, :], ALU.is_ge, ALU.mult).then_inc(a_done, 1)
                for u in range(2):
                    b = h * 2 + u
                    for t in range(BT):
                        dve.wait_ge(xa_done, b * BT + t + 1)
                        dve.wait_ge(x1_ps, 2 * BT + b * BT + t + 1)
                        dve.tensor_tensor(xb[:, u, t, :], xb[:, u, t, :], ps[:, t, :], ALU.add)
                        dve.drain().then_inc(x1_sb, 1)
                        dve.bn_stats(stat1[:, t, :], xb[:, u, t, :])
                        if u == 1 and t == 0:
                            norm_coefs(b - 1, 0)
                    dve.drain()
                    for t in range(BT):
                        dve.bn_aggr(mv1[:, u, t, :], stat1[:, t, :])
                    dve.drain().then_inc(x1_var, 1)
                norm_coefs(h * 2 + 1, 1)
            dve.wait_ge(log_sb, BATCH + 1)
            for i in range(T):
                dve.max(out=best[:, i, :], in_=logits[:, i, :])
            dve.drain()
            dve.tensor_tensor(gap[:], best[:, :, 0], best[:, :, 1], ALU.subtract)
            for i in range(T):
                dve.max_index(out=best_i[:, i, :], in_max=best[:, i, :], in_values=logits[:, i, :])
            dve.drain()
            dve.tensor_copy(idx_f[:], best_i[:, :, 0:PICKS])
            dve.drain().then_inc(gap_ok, 1)
            hot_g = hot.rearrange("p i k e -> p (i k) e")
            hot_wg = hot_w.rearrange("p i k e -> p (i k) e")
            dve.tensor_tensor(hot_g, iota_e[:, None, :].to_broadcast([P, GROUPS, E]),
                              idx_f[:].rearrange("p i k -> p (i k)")[:, :, None].to_broadcast([P, GROUPS, E]), ALU.is_equal)
            dve.drain()
            dve.tensor_tensor(member[:].rearrange("p (i e) -> p i e", i=T), hot[:, :, 0, :], hot[:, :, 1, :], ALU.add)
            dve.drain().then_inc(member_ok, 1)
            dve.tensor_tensor(hot_wg, hot_g, alpha_bc[:, None, :].to_broadcast([P, GROUPS, E]), ALU.mult)
            dve.drain()
            w_g = w_tok[:].rearrange("p i k -> p (i k)")
            dve.tensor_reduce(w_g, hot_wg, AX.X, ALU.add)
            dve.drain()
            dve.wait_ge(score_ok, 1)
            dve.scalar_tensor_tensor(w_g, score[:].rearrange("p i k -> p (i k)"), coef[:, 1:2], w_g, ALU.mult, ALU.mult)
            dve.wait_ge(rank_ps, 1)
            dve.tensor_copy(totals, ps[:, 5, 0:T * E].rearrange("p (i e) -> p e i", i=T))
            dve.drain()
            tot_f = totals.rearrange("p e i -> p (e i)")
            run_f = running.rearrange("p e i -> p (e i)")
            dve.tensor_tensor_scan(out=run_f, data0=ones[:], data1=tot_f, initial=0.0, op0=ALU.mult, op1=ALU.add)
            dve.drain()
            dve.tensor_tensor(start_e[:], running[:, :, 0], totals[:, :, 0], ALU.subtract)
            dve.drain()
            dve.tensor_tensor(count_e[:], running[:, :, T - 1], start_e[:], ALU.subtract)
            dve.drain()
            dve.tensor_tensor(run_f, run_f, tot_f, ALU.subtract)
            dve.tensor_tensor(tiles_cmp, count_e[:, :, None].to_broadcast([P, E, T]),
                              tile_starts[:, None, :].to_broadcast([P, E, T]), ALU.is_gt)
            dve.drain()
            dve.tensor_reduce(tiles_e[:], tiles_cmp, AX.X, ALU.add)
            dve.drain()
            dve.tensor_tensor_scan(out=tiles_end[:], data0=ones[:, 0:E], data1=tiles_e[:], initial=0.0,
                                   op0=ALU.mult, op1=ALU.add)
            dve.drain()
            dve.tensor_tensor(base_e[:], tiles_end[:], tiles_e[:], ALU.subtract)
            dve.tensor_tensor(exp_cmp, tiles_end[0:1, None, :].to_broadcast([1, TILES, E]),
                              iota_j[0:1, :, None].to_broadcast([1, TILES, E]), ALU.is_le)
            dve.drain()
            dve.tensor_reduce(exp_f[:], exp_cmp, AX.X, ALU.add)
            dve.scalar_tensor_tensor(base_e[:], base_e[:], float(P), start_e[:], ALU.mult, ALU.subtract)
            dve.drain()
            dve.tensor_scalar(exp_i[:], exp_f[:], float(E - 1), None, ALU.min)
            dve.tensor_tensor(place, running.rearrange("p e i -> p i e"),
                              base_e[:, None, :].to_broadcast([P, T, E]), ALU.add)
            dve.drain().then_inc(route_ok, 1)
            dve.tensor_tensor(place, place, ps[:, 4, 0:T * E].rearrange("p (i e) -> p i e", i=T), ALU.add)
            dve.drain()
            for k in range(PICKS):
                dve.tensor_tensor(hot_w[:, :, k, :], hot[:, :, k, :], place, ALU.mult)
            dve.drain()
            dve.tensor_reduce(pos[:], hot_wg, AX.X, ALU.add)
            dve.drain()
            dve.tensor_copy(pos_i[:], pos[:])
            dve.drain()
            dve.tensor_scalar(pos_q[:], pos_i[:], P - 1, None, ALU.bitwise_and)
            dve.tensor_scalar(pos_j[:], pos_i[:], P.bit_length() - 1, None, ALU.logical_shift_right)
            dve.drain()
            dve.tensor_copy(pos_qf[:], pos_q[:])
            dve.tensor_copy(pos_jf[:], pos_j[:])
            dve.drain()
            dve.tensor_tensor(slot_hot, iota_q[:, None, :].to_broadcast([P, GROUPS, P]),
                              pos_qf[:, :, None].to_broadcast([P, GROUPS, P]), ALU.is_equal)
            dve.tensor_tensor(tile_hot[:, :, 0, :], iota_j[:, None, :].to_broadcast([P, GROUPS, TILES]),
                              pos_jf[:, :, None].to_broadcast([P, GROUPS, TILES]), ALU.is_equal)
            dve.drain()
            for k in range(PICKS):
                dve.tensor_tensor(tile_hot[:, k:GROUPS:PICKS, 1, :], tile_hot[:, k:GROUPS:PICKS, 0, :],
                                  token_id[:, :, None].to_broadcast([P, T, TILES]), ALU.mult)
            dve.tensor_tensor(tile_hot[:, :, 2, :], tile_hot[:, :, 0, :],
                              w_g[:, :, None].to_broadcast([P, GROUPS, TILES]), ALU.mult)
            dve.drain().then_inc(hot_ok, 1)
            dve.wait_ge(table_ps, 1)
            dve.tensor_copy(table, ps[:, 7, 0:3 * TILES].rearrange("p (v j) -> p v j", v=3))
            dve.drain()
            dve.tensor_copy(src_idx[:, 0:TILES], table[:, 1, :])
            dve.tensor_copy(w_slot[:], table[:, 2, :])
            dve.tensor_scalar(table[:, 0, :], table[:, 0, :], -1.0, 1.0, ALU.mult, ALU.add)
            dve.drain()
            dve.scalar_tensor_tensor(dst_idx[:], table[:, 0, :], pad_row[:, 0:1], table[:, 1, :], ALU.mult, ALU.add)
            dve.drain().then_inc(slots_ok, 1)

            dve.wait_ge(b2_in_s, 16)

            def hidden(j, u):
                dve.wait_ge(hid_ps, j + 1)
                dve.tensor_copy(hid[u], ps[:, 2 + u, :]).then_inc(hid_sb, 1)

            def result(j, u):
                e = dve.value_load(exp_i[0:1, bass.ds(j, 1)], min_val=0, max_val=E - 1)
                dve.wait_ge(y_ps, j + 1)
                dve.tensor_tensor(yb[u], ps[:, 6 + u, :], b2_bc[:, bass.ds(e, 1), :].rearrange("p a n -> p (a n)"), ALU.add)
                dve.drain().then_inc(y_sb, 1)
                dve.wait_ge(rows_added, j + 1)
                dve.tensor_scalar(ys[u], yb[u], w_slot[:, bass.ds(j, 1)], None, ALU.mult).then_inc(ys_ready, 1)

            def transposed(j, u):
                dve.wait_ge(xgT_ps, j + 1)
                dve.tensor_copy(xgT[u], ps[:, u, :]).then_inc(xgT_sb, 1)

            transposed(0, 0)
            hidden(0, 0)
            transposed(1, 1)
            with dve.Fori(0, (TILES - 3) // 2) as jj:
                for u in range(2):
                    j = jj * 2 + u
                    hidden(j + 1, 1 - u)
                    transposed(j + 2, u)
                    result(j, u)
            for j in range(TILES - 3, TILES):
                if j + 1 < TILES:
                    hidden(j + 1, (j + 1) % 2)
                if j + 2 < TILES:
                    transposed(j + 2, j % 2)
                result(j, j % 2)

        @block.tensor
        def _(pe):
            pe.wait_ge(qk_in, 32)
            pe.wait_ge(consts, 2)
            pe.wait_ge(b1_in_s, 16)
            pe.transpose(ps[:, 3, 0:C], wq, ident[:])
            pe.transpose(ps[:, 3, C:2 * C], wk, ident[:])
            pe.transpose(ps[:, 3, 2 * C:2 * C + E * IB], b1_rows, ident[0:E * IB, 0:E * IB]).then_inc(wT_ps, 1)
            pe.wait_ge(wT_sb, 1)
            with pe.Fori(0, 2) as h:
                for u in range(2):
                    b = h * 2 + u
                    pe.wait_ge(ctx_in_s[u], 16 * h + 16)
                    pe.wait_ge(sim_sb, b * BT + BT)
                    for t in range(BT):
                        mm = pe.transpose(ps[:, 4 * u, t * P:(t + 1) * P], ctx_b[u][:, t * C:(t + 1) * C], ident[:])
                    mm.then_inc(ctxT_ps, 1)
                    pe.wait_ge(ctxT_sb, b + 1)
                    pe.matmul(ps[:, 4 * u + 1, :], wqT, ctxT[u], start=True, stop=True).then_inc(q_ps, 1)
                    pe.matmul(ps[:, 4 * u + 2, :], wkT, ctxT[u], start=True, stop=True).then_inc(k_ps, 1)
                    pe.wait_ge(qk_sb, b + 1)
                    for t in range(BT):
                        pe.matmul(ps[:, 4 * u + t, :], qT[u][:, t * P:(t + 1) * P], kT[u], start=True,
                                  stop=True).then_inc(sim_ps, 1)
            pe.wait_ge(bad_sb, 1)
            pe.wait_ge(sim_sb, 2 * BT + T)
            pe.matmul(ps[0:1, 7, 0:1], bad[:], ones[:, 0:1], start=True, stop=True).then_inc(bad_ps, 1)
            pe.wait_ge(const_in, 16)
            pe.wait_ge(coef_ok, 1)
            with pe.Fori(0, 2) as h:
                for u in range(2):
                    b = h * 2 + u
                    pe.wait_ge(a_done, b * BT + BT)
                    for t in range(BT):
                        pe.wait_ge(x1_sb, b * BT + t + 1)
                        pe.matmul(ps[:, t, :], ident_a[:], ab[:, u, t, :], start=True, stop=False)
                        for q in range(BT):
                            mm = pe.matmul(ps[:, t, q * P:(q + 1) * P], ab[:, u, q, t * P:(t + 1) * P], ident_a[:],
                                           start=False, stop=(q == BT - 1))
                        mm.then_inc(x1_ps, 1)
                for u in range(2):
                    b = h * 2 + u
                    for t in range(BT):
                        pe.wait_ge(xn_done, b * BT + t + 1)
                        if t >= 2:
                            pe.wait_ge(xnT_sb, b * BT + t - 1)
                        for k in range(KB):
                            mm = pe.transpose(ps[:, 4 + t % 2, k * P:(k + 1) * P], xnb[:, t, k * P:(k + 1) * P], ident[:])
                        mm.then_inc(xnT_ps, 1)
                        if t == 0:
                            pe.wait_ge(log_sb, b + 1)
                        pe.wait_ge(xnT_sb, b * BT + t + 1)
                        for k in range(KB):
                            mm = pe.matmul(ps[:, 6, t * E:(t + 1) * E], xnT[:, t % 2, k * P:(k + 1) * P], gate_w[:, k, :],
                                           start=(k == 0), stop=(k == KB - 1))
                        if t == BT - 1:
                            mm.then_inc(log_ps, 1)
            pe.wait_ge(member_ok, 1)
            pe.matmul(ps[:, 4, 0:T * E], before[:], member[:], start=True, stop=True)
            pe.matmul(ps[:, 5, 0:T * E], ones_b[:], member[:], start=True, stop=True).then_inc(rank_ps, 1)
            pe.wait_ge(hot_ok, 1)
            tile_hot_g = tile_hot.rearrange("p g v j -> p g (v j)")
            for g in range(GROUPS):
                mm = pe.matmul(ps[:, 7, 0:3 * TILES], slot_hot[:, g, :], tile_hot_g[:, g, :], start=(g == 0),
                               stop=(g == GROUPS - 1))
            mm.then_inc(table_ps, 1)

            pe.wait_ge(fc1_in, 16 * E)
            pe.wait_ge(fc2_in, 16 * E)
            pe.wait_ge(route_ok, 1)
            pe.wait_ge(slots_ok, 1)

            def expert(j):
                return pe.value_load(exp_i[0:1, bass.ds(j, 1)], min_val=0, max_val=E - 1)

            def w_block(e, m, k):
                return weights[:, bass.ds(e, 1), m, k, :].rearrange("p a n -> p (a n)")

            def turn_rows(u, arrivals):
                pe.wait_ge(gathered[u], arrivals)
                for k in range(KB):
                    mm = pe.transpose(ps[:, u, k * P:(k + 1) * P], xg[u][:, k * P:(k + 1) * P], ident[:])
                mm.then_inc(xgT_ps, 1)

            def layer1(j, u):
                e = expert(j)
                pe.wait_ge(xgT_sb, j + 1)
                for k in range(KB):
                    mm = pe.matmul(ps[:, 2 + u, :], xgT[u][:, k * P:(k + 1) * P], w_block(e, 0, k), start=(k == 0),
                                   stop=(k == KB - 1))
                mm.then_inc(hid_ps, 1)

            def turn_hidden(j, u):
                pe.wait_ge(hid_sb, j + 1)
                for i in range(IB):
                    mm = pe.transpose(ps[:, 4 + u, i * P:(i + 1) * P], hid[u][:, i * P:(i + 1) * P], ident[:])
                mm.then_inc(hidT_ps, 1)

            def layer2(j, u):
                e = expert(j)
                pe.wait_ge(gelu_sb, j + 1)
                pe.wait_ge(y_sb, j + 1)
                for i in range(IB):
                    mm = pe.matmul(ps[:, 6 + u, :], act_t[u][:, i * P:(i + 1) * P], w_block(e, 1, i), start=(i == 0),
                                   stop=(i == IB - 1))
                mm.then_inc(y_ps, 1)

            turn_rows(0, 16)
            layer1(0, 0)
            turn_rows(1, 16)
            with pe.Fori(0, (TILES - 3) // 2) as jj:
                for u in range(2):
                    j = jj * 2 + u
                    turn_hidden(j, u)
                    layer1(j + 1, 1 - u)
                    turn_rows(u, 16 * jj + 32)
                    layer2(j, u)
            for j in range(TILES - 3, TILES):
                turn_hidden(j, j % 2)
                if j + 1 < TILES:
                    layer1(j + 1, (j + 1) % 2)
                if j + 2 < TILES:
                    turn_rows(j % 2, 16 * (j // 2 + 2))
                layer2(j, j % 2)


_INS = ["x", "ctx_512", "g_xattn", "g_ffn", "L0_xattn_Wq", "L0_xattn_Wk", "L0_xattn_gamma_raw", "L0_ffn_gate_w",
        "L0_ffn_fc1_w", "L0_ffn_fc1_b", "L0_ffn_fc2_w", "L0_ffn_fc2_b", "L0_ffn_alpha"]


def kernel(**inputs):
    import concourse.bacc as bacc
    from concourse.bass_utils import run_bass_kernel_spmd as run

    nc = bacc.Bacc("TRN2", target_bir_lowering=False, num_devices=1, dynamic_dma_scratch_size=8192)
    arrays, args = {}, []
    for name in _INS:
        a = np.ascontiguousarray(inputs[name])
        if name in ("x", "ctx_512"):
            a = a.reshape(TOKENS, -1)
        if a.ndim == 0:
            a = a.reshape(1)
        arrays[f"in_{name}"] = a
        args.append(nc.dram_tensor(f"in_{name}", a.shape, mybir.dt.from_np(a.dtype), kind="ExternalInput").ap())
    xn_rows = nc.dram_tensor("xn_rows", (TOKENS, D), F32, kind="Internal").ap()
    out_rows = nc.dram_tensor("out_rows", (TOKENS + P, D), F32, kind="ExternalOutput").ap()
    build(nc, *args, xn_rows, out_rows)
    r = run(nc, [arrays], core_ids=[0])
    return r.results[0]["out_rows"][:TOKENS].reshape(BATCH, SEQ, D)
```

```python
import math
from contextlib import ExitStack

import concourse.bass as bass
import numpy as np
from concourse import mybir

F32 = mybir.dt.float32
BF16 = mybir.dt.bfloat16
I32 = mybir.dt.int32
U32 = mybir.dt.uint32
ALU = mybir.AluOpType
ACT = mybir.ActivationFunctionType
AX = mybir.AxisListType

P = 128
BATCH, SEQ, D = 4, 512, 512
C = 128
HEADS = 4
E = 8
PICKS = 2
INTER = 512
TOKENS = BATCH * SEQ
T = TOKENS // P
BT = SEQ // P
KB = D // P
IB = INTER // P
TOPK = int(SEQ * 0.3)
GROUPS = T * PICKS
TILES = (TOKENS * PICKS + E * (P - 1)) // P
MAIN_TILES = TOKENS * PICKS // P + E // 2
CHUNKS = 4
LN_EPS = 1e-5
SIM_SCALE = float(np.float32(1.0) / (np.sqrt(np.float32(C // HEADS)) * np.float32(HEADS)))

SIM_BANKS = (0, 1, 6, 7)
ROUNDS = 5
T_DVE = 8
WINDOW = 8
BELOW = SEQ - TOPK
AIM = BELOW + WINDOW / 2
START_SIGMAS = 0.55
DENSITY = 0.35
LOW_SIGMAS, HIGH_SIGMAS = -0.45, 1.55
CLIP = 0.03
SQRT_MAGIC = 532487669.0
BUSY_LOADS, BUSY_PROOF, BUSY_SLOTS, BUSY_GATHER = 60, 36, 84, 60
AHEAD = 4
BIG = 2.0 ** 100
MOST, SPAN = 2.0 ** 27, 2.0 ** 70
LOWEST = -3e38


def dve_subtracts(i):
    return i % 3 == 0


def not_above(sigmas):
    return SEQ * (1.0 - 0.5 * math.erfc(sigmas / math.sqrt(2.0)))


def build(nc, x, ctx_in, g_x, g_f, wq_in, wk_in, gam_in, gate_in, fc1, b1_in, fc2, b2_in, alpha_in, xn_rows, out_rows):
    es = ExitStack()
    with es:
        def sb(name, shape, dt=F32):
            return es.enter_context(nc.sbuf_tensor(name, shape, dt))

        def sem(name):
            return es.enter_context(nc.semaphore(name))

        weights = sb("weights", [P, E, 2, KB, INTER])
        sim = sb("sim", [P, T, SEQ])
        xb = sb("xb", [P, 2, BT, D])
        ab = sb("ab", [P, 2, BT, SEQ])
        xnb = sb("xnb", [P, BT, D])
        xnT = sb("xnT", [P, 2, D])
        ab_flat = ab[:].rearrange("p u t n -> p (u t n)")
        sim_flat = sim[:].rearrange("p t n -> p (t n)")

        def sequences(region):
            return [region[:, b * SEQ:(b + 1) * SEQ] for b in range(BATCH)]

        room = [weights[:, e, m].rearrange("p k n -> p (k n)") for e in (E - 2, E - 1) for m in range(2)]
        ctx_b, ctxT, qT, kT = (sequences(r) for r in room)
        slot_hot = sim_flat[:, 0:GROUPS * P].rearrange("p (g q) -> p g q", g=GROUPS)
        tile_hot = ab_flat[:, 0:GROUPS * TILES].rearrange("p (g j) -> p g j", g=GROUPS)
        tile_val = ab_flat[:, GROUPS * TILES:GROUPS * 3 * TILES].rearrange("p (g v j) -> p g v j", g=GROUPS, v=2)
        b2_bc = xb[:].rearrange("p u t n -> p (u t n)").rearrange("p (e n) -> p e n", e=E)

        def carve(region, at, *sizes):
            starts = [at + sum(sizes[:n]) for n in range(len(sizes))]
            return [region[:, start:start + size] for start, size in zip(starts, sizes)]

        rings = carve(sim_flat, 0, *[D] * 12)
        xg, xgT, hid, act_t, yb, ys = (rings[n:n + 2] for n in range(0, 12, 2))
        hot, hot_w, totals, running, tiles_cmp, place, exp_cmp, table, empty = carve(
            sim_flat, 12 * D, GROUPS * E, GROUPS * E, T * E, T * E, T * E, T * E, TILES * E, 2 * TILES, TILES)
        hot, hot_w = (v.rearrange("p (i k e) -> p i k e", k=PICKS, e=E) for v in (hot, hot_w))
        totals, running, tiles_cmp = (v.rearrange("p (e i) -> p e i", e=E) for v in (totals, running, tiles_cmp))
        place = place.rearrange("p (i e) -> p i e", e=E)
        exp_cmp = exp_cmp[0:1].rearrange("p (j e) -> p j e", e=E)
        table = table.rearrange("p (v j) -> p v j", v=2)

        wq, wk, wqT, wkT, b1_rows, top, pick, pad_zero = carve(
            xnb[:].rearrange("p t n -> p (t n)"), 0, C, C, C, C, P, T * WINDOW, T * WINDOW, D)
        b1_rows = b1_rows[0:E * IB]
        top, pick = (v.rearrange("p (i w) -> p i w", w=WINDOW) for v in (top, pick))
        junk = ab_flat.bitcast(BF16).rearrange("p (i n) -> p i n", i=T)
        penal = [ab[:, 1, t, :] for t in range(BT)] + [xnT[:, u, :] for u in range(2)]

        def logT(b):
            return sim[0:E, b * BT + 1, :]

        ident = sb("ident", [P, P])
        ident_a = sb("ident_a", [P, P])
        before = sb("before", [P, P], BF16)
        ones_b = sb("ones_b", [P, P], BF16)
        ones = sb("ones", [P, T * E])
        gate_w = sb("gate_w", [P, KB, E])
        b1T = sb("b1T", [P, E * IB])
        raw = sb("raw", [P, 3])
        alpha_bc = sb("alpha_bc", [P, E])
        coef = sb("coef", [P, 8])
        gates, gamma, one_less_gamma = coef[:, 0:2], coef[:, 2:3], coef[:, 5:6]
        tanh_gx, tanh_gf = coef[:, 0:1], coef[:, 1:2]
        c_norm, c_a = coef[:, 3:4], coef[:, 4:5]
        iota_e = sb("iota_e", [P, E])
        iota_q = sb("iota_q", [P, P])
        iota_j = sb("iota_j", [P, TILES])
        tile_starts = sb("tile_starts", [P, T])
        token_1 = sb("token_1", [P, T])
        pad_row_1 = sb("pad_row_1", [P, 1])

        stats = sb("stats", [P, T, 6])
        mv = sb("mv", [P, T, 2])
        dev = sb("dev", [P, T])
        t_now = sb("t_now", [P, T])
        hi_big = sb("hi_big", [P, T])
        cnt = sb("cnt", [P, T])
        lo = sb("lo", [P, T])
        hi = sb("hi", [P, T])
        n_lo = sb("n_lo", [P, T])
        n_hi = sb("n_hi", [P, T])
        most, aim, unit = (sb(n, [P, T]) for n in ("most", "aim", "unit"))
        neg_half = sb("neg_half", [P, T])
        span = sb("span", [P, T])
        fits = sb("fits", [P, T])
        matched = sb("matched", [P, T])
        var_x = sb("var_x", [P, T])
        width = sb("width", [P, T])
        over = sb("over", [P, T], I32)
        under = sb("under", [P, T], I32)
        tmp0 = sb("tmp0", [P, T])
        tmp1 = sb("tmp1", [P, T])
        thr = sb("thr", [P, T])
        proved = sb("proved", [P, 1])
        proved_i = sb("proved_i", [1, 1], I32)
        work = sb("work", [P, 8])

        statx = sb("statx", [P, T, 6])
        mvx = sb("mvx", [P, T, 2])
        rstd_x = sb("rstd_x", [P, T])
        xa_scale = sb("xa_scale", [P, T])
        xa_bias = sb("xa_bias", [P, T])
        stat1 = sb("stat1", [P, BT, 6])
        mv1 = sb("mv1", [P, 2, BT, 2])
        var1 = sb("var1", [P, BT])
        xn_scale = sb("xn_scale", [P, 2, BT])
        xn_bias = sb("xn_bias", [P, 2, BT])

        logits = sb("logits", [P, T, E])
        best = sb("best", [P, T, E])
        best_i = sb("best_i", [P, T, E], U32)
        idx_f = sb("idx_f", [P, T, PICKS])
        member = sb("member", [P, T * E], BF16)
        gap = sb("gap", [P, T])
        score = sb("score", [P, T, PICKS])
        w_tok = sb("w_tok", [P, T, PICKS])
        count_e = sb("count_e", [P, E])
        start_e = sb("start_e", [P, E])
        tiles_e = sb("tiles_e", [P, E])
        tiles_end = sb("tiles_end", [P, E])
        base_e = sb("base_e", [P, E])
        pos = sb("pos", [P, GROUPS])
        pos_j = sb("pos_j", [P, GROUPS], I32)
        pos_qf = sb("pos_qf", [P, GROUPS])
        pos_jf = sb("pos_jf", [P, GROUPS])
        exp_f = sb("exp_f", [1, TILES])
        exp_i = sb("exp_i", [1, TILES], I32)
        used_i = sb("used_i", [1, 1], I32)
        w_slot = sb("w_slot", [P, TILES])
        src_idx = sb("src_idx", [P, TILES], U32)
        dst_idx = sb("dst_idx", [P, TILES], U32)
        src_now = sb("src_now", [P, 2], U32)
        dst_now = sb("dst_now", [P, 2], U32)

        ps = es.enter_context(nc.psum_tensor("ps", [P, 8, 512], F32))

        const_in, qk_in, b1_in_s, scal_in = sem("const_in"), sem("qk_in"), sem("b1_in_s"), sem("scal_in")
        ctx_in_s = [sem(f"ctx_in{b}") for b in range(BATCH)]
        x_in = [sem("x_in0"), sem("x_in1")]
        fc1_in, fc2_in, b2_in_s = sem("fc1_in"), sem("fc2_in"), sem("b2_in_s")
        consts = sem("consts")
        wT_ps, wT_sb = sem("wT_ps"), sem("wT_sb")
        coef_ok = sem("coef_ok")
        ctxT_ps, ctxT_sb, q_ps, k_ps, qk_sb = (sem(n) for n in ("ctxT_ps", "ctxT_sb", "q_ps", "k_ps", "qk_sb"))
        sim_ps, sim_sb = sem("sim_ps"), sem("sim_sb")
        trial, counted, pen_done, pen_used = sem("trial"), sem("counted"), sem("pen_done"), sem("pen_used")
        proved_sb, proved_ps = sem("proved_sb"), sem("proved_ps")
        act_coef, sig_done, a_done, xa_done = sem("act_coef"), sem("sig_done"), sem("a_done"), sem("xa_done")
        parked_read, var_ok, rstd_ok = sem("parked_read"), sem("var_ok"), sem("rstd_ok")
        x1_var, x1_rstd, pen_less = sem("x1_var"), sem("x1_rstd"), sem("pen_less")
        x_parked = [sem("x_parked0"), sem("x_parked1")]
        x1_ps, x1_sb, xn_done = (sem(n) for n in ("x1_ps", "x1_sb", "xn_done"))
        xnT_ps, xnT_sb, gate_ps, logT_sb, log_ps, log_sb = (
            sem(n) for n in ("xnT_ps", "xnT_sb", "gate_ps", "logT_sb", "log_ps", "log_sb"))
        xn_out, x1_out, pad_out = sem("xn_out"), sem("x1_out"), sem("pad_out")
        gap_ok, score_ok, member_ok, rank_ps, tile_ok, value_ok, hot_ok, table_ps, route_ok, src_ok, dst_ok = (
            sem(n) for n in ("gap_ok", "score_ok", "member_ok", "rank_ps", "tile_ok", "value_ok", "hot_ok", "table_ps",
                             "route_ok", "src_ok", "dst_ok"))
        src_set, dst_set, pool_turn, rows_added = sem("src_set"), sem("dst_set"), sem("pool_turn"), sem("rows_added")
        gathered = [sem("gathered0"), sem("gathered1")]
        scattered = [sem("scattered0"), sem("scattered1")]
        xgT_ps, xgT_sb, hid_ps, hid_sb, hidT_ps, gelu_sb, y_ps, y_sb, ys_ready = (
            sem(n) for n in ("xgT_ps", "xgT_sb", "hid_ps", "hid_sb", "hidT_ps", "gelu_sb", "y_ps", "y_sb", "ys_ready"))

        ctx_v = ctx_in.rearrange("(b t p) c -> b p t c", t=BT, p=P)
        x_v = x.rearrange("(b t p) n -> b p t n", t=BT, p=P)
        xn_v = xn_rows.rearrange("(b t p) n -> b p t n", t=BT, p=P)
        out_v = out_rows[0:TOKENS, :].rearrange("(b t p) n -> b p t n", t=BT, p=P)

        def bc_row(v, n):
            return v.rearrange("(a b) -> a b", a=1).to_broadcast([P, n])

        chunk = [slice(c * GROUPS // CHUNKS, (c + 1) * GROUPS // CHUNKS) for c in range(CHUNKS)]
        w_tok_g = w_tok[:].rearrange("p i k -> p (i k)")

        block = es.enter_context(nc.Block())

        @block.sync
        def _(sp):
            sp.dma_start(wq, wq_in).then_inc(qk_in, 16)
            sp.dma_start(wk, wk_in).then_inc(qk_in, 16)
            for b in range(BATCH):
                sp.dma_start(ctx_b[b].rearrange("p (t c) -> p t c", t=BT), ctx_v[b]).then_inc(ctx_in_s[b], 16)
            for n, g in enumerate((g_x, g_f, gam_in)):
                sp.dma_start(raw[:, n:n + 1], bc_row(g, 1)).then_inc(scal_in, 16)
            sp.dma_start(alpha_bc[:], bc_row(alpha_in, E)).then_inc(scal_in, 16)
            sp.dma_start(b1_rows, b1_in.rearrange("e (i p) -> (e i) p", p=P)).then_inc(b1_in_s, 16)
            sp.dma_start(gate_w[:], gate_in.rearrange("(k p) e -> p k e", p=P)).then_inc(const_in, 16)
            for u in range(2):
                sp.dma_start(sim[:, (2 + u) * BT:(3 + u) * BT], x_v[2 + u]).then_inc(x_parked[u], 16)
            for u in range(2):
                sp.dma_start(xb[:, u], x_v[u]).then_inc(x_in[u], 16)
            for e in range(E):
                if e == E - 2:
                    sp.wait_ge(sim_ps, T)
                for m, (fc, s) in enumerate(((fc1, fc1_in), (fc2, fc2_in))):
                    sp.dma_start(weights[:, e, m], fc[e].rearrange("(k p) n -> p k n", p=P)).then_inc(s, 16)
            sp.wait_ge(consts, 1)
            sp.dma_start(out_rows[TOKENS:TOKENS + P, :], pad_zero).then_inc(pad_out, 16)
            for b in range(BATCH):
                u = b % 2
                sp.wait_ge(x1_sb, BT * (b + 1))
                sp.dma_start(out_v[b], xb[:, u]).then_inc(x1_out, 16)
                sp.wait_ge(xn_done, BT * (b + 1))
                sp.dma_start(xn_v[b], xnb[:]).then_inc(xn_out, 16)
                if b + 2 < BATCH:
                    sp.wait_ge(x1_out, 16 * (b + 1))
                    sp.dma_start(xb[:, u], x_v[b + 2]).then_inc(x_in[u], 16)
            sp.wait_ge(x1_out, 16 * BATCH)
            sp.dma_start(b2_bc, b2_in.rearrange("(a e) n -> a e n", a=1).to_broadcast([P, E, D])).then_inc(b2_in_s, 16)

        @block.gpsimd
        def _(pool):
            pool.memset(pad_zero, 0.0).then_inc(consts, 1)
            pool.memset(ident[:], 0.0)
            pool.memset(ones_b[:], 1.0)
            pool.memset(ones[:], 1.0)
            pool.drain()
            pool.affine_select(out=ident[:], in_=ident[:], compare_op=ALU.not_equal, fill=1.0, base=0,
                               pattern=[[-1, P]], channel_multiplier=1).then_inc(consts, 1)
            pool.affine_select(out=before[:], in_=ones_b[:], compare_op=ALU.is_gt, fill=0.0, base=0,
                               pattern=[[1, P]], channel_multiplier=-1)
            for buf, pattern, base, by in (
                (iota_e[:], [[1, E]], 0, 0), (iota_q[:], [[1, P]], 0, 0), (iota_j[:], [[1, TILES]], 0, 0),
                (tile_starts[:], [[P, T]], 0, 0), (token_1[:], [[P, T]], 1, 1), (pad_row_1[:], [[1, 1]], TOKENS + 1, 1),
            ):
                pool.iota(buf, pattern, base=base, channel_multiplier=by, allow_small_or_imprecise_dtypes=True)
            for cols, n_of, step in ((slice(0, T_DVE), lambda n: float(n), 1.0),
                                     (slice(T_DVE, T), lambda n: float(2 * n - SEQ), 0.5)):
                pool.memset(most[:, cols], n_of(BELOW))
                pool.memset(aim[:, cols], n_of(AIM))
                pool.memset(n_lo[:, cols], n_of(not_above(LOW_SIGMAS)))
                pool.memset(n_hi[:, cols], n_of(not_above(HIGH_SIGMAS)))
                pool.memset(unit[:, cols], step / (SEQ * DENSITY))
            pool.memset(neg_half[:], -0.5)
            pool.drain().then_inc(consts, 1)

            pool.wait_ge(var_ok, 1)
            pool.tensor_tensor(rstd_x[:], var_x[:], neg_half[:], ALU.pow)
            pool.drain().then_inc(rstd_ok, 1)
            for i in range(T):
                if not dve_subtracts(i):
                    pool.wait_ge(pen_done, i + 1)
                    pool.tensor_tensor(penal[i % len(penal)], sim[:, i, :], penal[i % len(penal)],
                                       ALU.subtract).then_inc(pen_less, 1)
            with pool.Fori(0, 2) as h:
                for u in range(2):
                    pool.wait_ge(x1_var, h * 2 + u + 1)
                    pool.sem_inc(pool_turn, 1)
                    pool.tensor_scalar(var1[:], mv1[:, u, :, 1], LN_EPS, None, ALU.add)
                    pool.drain()
                    pool.tensor_tensor(xn_scale[:, u, :], var1[:], neg_half[:, 0:BT], ALU.pow)
                    pool.drain().then_inc(x1_rstd, 1)
            for c in range(CHUNKS):
                pool.wait_ge(tile_ok, c + 1)
                for k in range(PICKS):
                    picks = slice(chunk[c].start + k, chunk[c].stop, PICKS)
                    pool.tensor_tensor(tile_val[:, picks, 0, :], tile_hot[:, picks, :],
                                       token_1[:, c * T // CHUNKS:(c + 1) * T // CHUNKS, None].to_broadcast(
                                           [P, T // CHUNKS, TILES]), ALU.mult)
                pool.drain()
                pool.tensor_tensor(tile_val[:, chunk[c], 1, :], tile_hot[:, chunk[c], :],
                                   w_tok_g[:, chunk[c], None].to_broadcast([P, GROUPS // CHUNKS, TILES]),
                                   ALU.mult).then_inc(value_ok, 1)

            pool.wait_ge(xn_out, 16 * BATCH)
            pool.wait_ge(src_ok, 1)

            last_token, last_row = pool.to_reg(TOKENS - 1), pool.to_reg(TOKENS + P - 1)

            def gather(j, u):
                pool.tensor_copy(src_now[:, u:u + 1], src_idx[:, bass.ds(j, 1)]).then_inc(src_set, 1)
                pool.wait_ge(src_set, j + 1)
                pool.sem_inc(pool_turn, 1)
                pool.indirect_dma_start(
                    out=xg[u], out_offset=None, in_=xn_rows,
                    in_offset=bass.IndirectOffsetOnAxis(ap=src_now[:, u:u + 1], axis=0),
                    bounds_check=last_token).then_inc(gathered[u], 16)

            def scatter(j, u):
                pool.tensor_copy(dst_now[:, u:u + 1], dst_idx[:, bass.ds(j, 1)]).then_inc(dst_set, 1)
                pool.wait_ge(dst_set, j + 1)
                pool.wait_ge(ys_ready, j + 1)
                pool.sem_inc(pool_turn, 1)
                pool.indirect_dma_start(
                    out=out_rows, out_offset=bass.IndirectOffsetOnAxis(ap=dst_now[:, u:u + 1], axis=0),
                    in_=ys[u], in_offset=None, bounds_check=last_row,
                    compute_op=ALU.add).then_inc(scattered[u], 16)

            def added(u, scatters):
                pool.wait_ge(scattered[u], scatters)
                pool.sem_inc(rows_added, 1)

            def move_rows(first, tiles):
                for j in range(first, min(first + AHEAD, first + tiles)):
                    if j >= first + 2:
                        pool.wait_ge(xgT_ps, j - 1)
                    gather(j, j % 2)
                    if j == first + 1 and first == 0:
                        pool.wait_ge(dst_ok, 1)
                        pool.wait_ge(x1_out, 16 * BATCH)
                        pool.wait_ge(pad_out, 16)
                looped = max(tiles - AHEAD, 0) // 2
                if looped:
                    with pool.Fori(first // 2, first // 2 + looped) as jj:
                        for u in range(2):
                            j = jj * 2 + u
                            scatter(j, u)
                            pool.wait_ge(xgT_ps, j + AHEAD - 1)
                            gather(j + AHEAD, u)
                            added(u, 16 * jj + 16)
                for j in range(first + looped * 2, first + tiles):
                    scatter(j, j % 2)
                    if j + AHEAD < first + tiles:
                        pool.wait_ge(xgT_ps, j + AHEAD - 1)
                        gather(j + AHEAD, j % 2)
                    added(j % 2, 16 * (j // 2 + 1))

            move_rows(0, MAIN_TILES)
            used = pool.value_load(used_i[0:1, 0:1], min_val=0, max_val=TILES)
            with pool.If(used > MAIN_TILES):
                move_rows(MAIN_TILES, TILES - MAIN_TILES)
            with pool.Else():
                pool.drain()

        @block.scalar
        def _(act):
            act.wait_ge(scal_in, 64)
            act.activation(gates, raw[:, 0:2], ACT.Tanh)
            act.activation(gamma, raw[:, 2:3], ACT.Sigmoid).then_inc(act_coef, 1)
            act.wait_ge(qk_in, 32)
            act.wait_ge(wT_ps, 1)
            act.copy(wqT, ps[:, 3, 0:C])
            act.copy(wkT, ps[:, 3, C:2 * C])
            act.copy(b1T[:], ps[:, 3, 2 * C:2 * C + E * IB])
            act.drain().then_inc(wT_sb, 1)
            def context(b):
                act.wait_ge(ctxT_ps, b + 1)
                act.copy(ctxT[b], ps[:, b % 2, :]).then_inc(ctxT_sb, 1)

            context(0)
            for b in range(BATCH):
                if b + 1 < BATCH:
                    context(b + 1)
                act.wait_ge(q_ps, b + 1)
                act.copy(qT[b], ps[:, 2 + b % 2, :]).then_inc(qk_sb, 1)
                act.wait_ge(k_ps, b + 1)
                act.copy(kT[b], ps[:, 4 + b % 2, :]).then_inc(qk_sb, 1)
            for i in range(T):
                if i == 2 * BT:
                    act.wait_ge(parked_read, 1)
                act.wait_ge(sim_ps, i + 1)
                act.activation(sim[:, i, :], ps[:, SIM_BANKS[i % 4], :], ACT.Copy, scale=SIM_SCALE).then_inc(sim_sb, 1)
            act.drain()

            def sign_sums():
                for i in range(T_DVE, T):
                    last = act.activation(junk[:, i, :], sim[:, i, :], ACT.Sign, bias=t_now[:, i:i + 1], scale=-1.0,
                                          accum_out=cnt[:, i:i + 1])
                last.then_inc(counted, 1)
                act.drain()

            with act.Fori(0, ROUNDS) as r:
                act.wait_ge(trial, r + 1)
                sign_sums()
            act.wait_ge(trial, ROUNDS + 1)
            for i in range(T):
                if i >= len(penal):
                    act.wait_ge(pen_used, i + 1 - len(penal))
                act.activation(penal[i % len(penal)], sim[:, i, :], ACT.Relu, bias=hi_big[:, i:i + 1],
                               scale=BIG).then_inc(pen_done, 1)
            act.wait_ge(coef_ok, 2)

            def sigmoids(b):
                if b >= 2:
                    act.wait_ge(x1_ps, BT * (b - 1))
                for t in range(BT):
                    act.activation(ab[:, b % 2, t, :], sim[:, b * BT + t, :], ACT.Sigmoid).then_inc(sig_done, 1)

            def affine_x(b):
                act.wait_ge(x_in[b % 2], 16 * (b // 2 + 1))
                for t in range(BT):
                    i = b * BT + t
                    act.activation(xb[:, b % 2, t, :], xb[:, b % 2, t, :], ACT.Identity, scale=xa_scale[:, i:i + 1],
                                   bias=xa_bias[:, i:i + 1]).then_inc(xa_done, 1)

            def finish_logits(b):
                act.wait_ge(log_ps, b + 1)
                act.copy(logits[:, b * BT:(b + 1) * BT, :].rearrange("p t e -> p (t e)"),
                         ps[:, 7, 0:BT * E]).then_inc(log_sb, 1)

            sigmoids(0)
            affine_x(0)
            act.wait_ge(pen_used, T)
            sigmoids(1)
            affine_x(1)
            for b in range(BATCH):
                if b + 2 < BATCH:
                    sigmoids(b + 2)
                if b >= 1:
                    finish_logits(b - 1)
                for t in range(BT):
                    act.wait_ge(xnT_ps, b * BT + t + 1)
                    if b * BT + t >= 2:
                        act.wait_ge(gate_ps, b * BT + t - 1)
                    act.copy(xnT[:, t % 2, :], ps[:, 4 + t % 2, :]).then_inc(xnT_sb, 1)
                act.wait_ge(gate_ps, (b + 1) * BT)
                act.copy(logT(b), ps[0:E, 6, :]).then_inc(logT_sb, 1)
                if b + 2 < BATCH:
                    affine_x(b + 2)
            finish_logits(BATCH - 1)
            act.wait_ge(gap_ok, 1)
            act.activation(score[:, :, 0], gap[:], ACT.Sigmoid)
            act.activation(score[:, :, 1], gap[:], ACT.Sigmoid, scale=-1.0).then_inc(score_ok, 1)

            act.wait_ge(route_ok, 1)

            def gelu(j, u):
                e = act.value_load(exp_i[0:1, bass.ds(j, 1)], min_val=0, max_val=E - 1)
                act.wait_ge(hidT_ps, j + 1)
                for i in range(IB):
                    last = act.activation(act_t[u][:, i * P:(i + 1) * P], ps[:, 4 + u, i * P:(i + 1) * P], ACT.Gelu,
                                          bias=b1T[:, bass.ds(e * IB + i, 1)])
                last.then_inc(gelu_sb, 1)

            with act.Fori(0, MAIN_TILES // 2) as jj:
                for u in range(2):
                    gelu(jj * 2 + u, u)
            used = act.value_load(used_i[0:1, 0:1], min_val=0, max_val=TILES)
            with act.If(used > MAIN_TILES):
                for j in range(MAIN_TILES, TILES):
                    gelu(j, j % 2)
            with act.Else():
                act.drain()

        @block.vector
        def _(dve):
            dve.wait_ge(act_coef, 1)
            dve.tensor_scalar(one_less_gamma, gamma, -1.0, 1.0, ALU.mult, ALU.add)
            dve.tensor_scalar(c_a, gamma, tanh_gx, 0.5, ALU.mult, ALU.mult)
            dve.drain()
            dve.tensor_tensor(c_norm, one_less_gamma, tanh_gx, ALU.mult)
            dve.wait_ge(consts, 3)
            dve.tensor_scalar(ident_a[:], ident[:], c_a, None, ALU.mult)
            dve.drain().then_inc(coef_ok, 1)
            dve.sem_inc(y_sb, 2)
            dve.sem_inc(rows_added, 2)

            for u in range(2):
                dve.wait_ge(x_parked[u], 16)
                for t in range(BT):
                    i = (2 + u) * BT + t
                    last = dve.bn_stats(statx[:, i, :], sim[:, i, :])
            last.then_inc(parked_read, 1)
            for u in range(2):
                dve.wait_ge(x_in[u], 16)
                for t in range(BT):
                    dve.bn_stats(statx[:, u * BT + t, :], xb[:, u, t, :])
            dve.drain()
            for i in range(T):
                dve.bn_aggr(mvx[:, i, :], statx[:, i, :])
            dve.drain()
            dve.tensor_scalar(var_x[:], mvx[:, :, 1], LN_EPS, None, ALU.add)
            dve.drain().then_inc(var_ok, 1)
            for i in range(T):
                dve.wait_ge(sim_sb, i + 1)
                dve.bn_stats(stats[:, i, :], sim[:, i, :])
                if i % BT == BT - 1:
                    dve.drain()
                    for k in range(i + 1 - BT, i + 1):
                        dve.bn_aggr(mv[:, k, :], stats[:, k, :])
            dve.drain()
            mean = mv[:, :, 0]
            dve.tensor_scalar(over[:], mv[:, :, 1].bitcast(I32), 1, None, ALU.logical_shift_right)
            dve.drain()
            dve.tensor_scalar(dev[:].bitcast(I32), over[:], SQRT_MAGIC, None, ALU.add)
            dve.drain()
            dve.scalar_tensor_tensor(t_now[:], dev[:], START_SIGMAS, mean, ALU.mult, ALU.add)
            dve.drain().then_inc(trial, 1)
            dve.scalar_tensor_tensor(lo[:], dev[:], LOW_SIGMAS, mean, ALU.mult, ALU.add)
            dve.scalar_tensor_tensor(hi[:], dev[:], HIGH_SIGMAS, mean, ALU.mult, ALU.add)
            dve.tensor_tensor(dev[:], dev[:], unit[:], ALU.mult)

            def count(rounds):
                for i in range(T_DVE):
                    dve.tensor_scalar(junk[:, i, :], sim[:, i, :], t_now[:, i:i + 1], None, ALU.is_le, ALU.add,
                                      accum_out=cnt[:, i:i + 1])
                dve.drain()
                dve.wait_ge(counted, rounds)

            def narrow():
                dve.tensor_tensor(over[:], cnt[:], most[:], ALU.is_le)
                dve.tensor_tensor(under[:], cnt[:], most[:], ALU.is_gt)
                dve.drain()
                dve.copy_predicated(lo[:], over[:], t_now[:])
                dve.copy_predicated(n_lo[:], over[:], cnt[:])
                dve.copy_predicated(hi[:], under[:], t_now[:])
                dve.copy_predicated(n_hi[:], under[:], cnt[:])

            count(1)
            narrow()
            dve.tensor_tensor(tmp0[:], aim[:], cnt[:], ALU.subtract)
            dve.drain()
            dve.tensor_tensor(tmp1[:], tmp0[:], dev[:], ALU.mult)
            dve.drain()
            dve.tensor_tensor(t_now[:], t_now[:], tmp1[:], ALU.add)
            dve.drain().then_inc(trial, 1)
            for r in range(1, ROUNDS - 1):
                count(r + 1)
                narrow()
                dve.drain()
                dve.tensor_tensor(tmp0[:], n_hi[:], n_lo[:], ALU.subtract)
                dve.tensor_tensor(tmp1[:], n_hi[:], aim[:], ALU.subtract)
                dve.tensor_tensor(width[:], lo[:], hi[:], ALU.subtract)
                dve.drain()
                dve.scalar_tensor_tensor(tmp1[:], tmp0[:], CLIP, tmp1[:], ALU.mult, ALU.max)
                dve.reciprocal(cnt[:], tmp0[:])
                dve.drain()
                dve.tensor_tensor(tmp1[:], tmp1[:], cnt[:], ALU.mult)
                dve.drain()
                dve.scalar_tensor_tensor(tmp1[:], tmp1[:], 1.0 - CLIP, width[:], ALU.min, ALU.mult)
                dve.drain()
                dve.tensor_tensor(t_now[:], tmp1[:], hi[:], ALU.add)
                dve.drain().then_inc(trial, 1)
            count(ROUNDS)
            narrow()
            dve.drain()
            dve.tensor_scalar(hi_big[:], hi[:], -BIG, None, ALU.mult)
            dve.drain().then_inc(trial, 1)
            dve.wait_ge(rstd_ok, 1)
            dve.tensor_scalar(tmp0[:], rstd_x[:], c_norm, None, ALU.mult)
            dve.drain()
            dve.tensor_scalar(xa_scale[:], tmp0[:], 1.0, None, ALU.add)
            dve.scalar_tensor_tensor(xa_bias[:], tmp0[:], -1.0, mvx[:, :, 0], ALU.mult, ALU.mult)
            dve.drain().then_inc(coef_ok, 1)
            dve.tensor_scalar(tmp0[:, 0:T_DVE], n_hi[:, 0:T_DVE], float(TOPK - 1 - SEQ), None, ALU.add)
            dve.tensor_scalar(tmp0[:, T_DVE:T], n_hi[:, T_DVE:T], 0.5, TOPK - 1 - SEQ / 2, ALU.mult, ALU.add)
            dve.scalar_tensor_tensor(tmp1[:], hi[:], -1.0, hi[:], ALU.mult, ALU.max)
            dve.drain()
            dve.tensor_tensor(pick, iota_e[:, None, :].to_broadcast([P, T, WINDOW]),
                              tmp0[:, :, None].to_broadcast([P, T, WINDOW]), ALU.is_equal)
            dve.tensor_scalar(span[:], tmp1[:], SPAN, None, ALU.mult)
            dve.tensor_scalar(fits[:], tmp1[:], MOST, None, ALU.is_lt)
            dve.drain()
            dve.tensor_reduce(matched[:], pick, AX.X, ALU.add)
            dve.drain()
            dve.tensor_tensor(fits[:], fits[:], matched[:], ALU.mult)
            for i in range(T):
                dve.wait_ge(pen_done, i + 1)
                if dve_subtracts(i):
                    dve.tensor_tensor(penal[i % len(penal)], sim[:, i, :], penal[i % len(penal)], ALU.subtract)
                    dve.drain()
                else:
                    dve.wait_ge(pen_less, sum(not dve_subtracts(k) for k in range(i + 1)))
                dve.max(out=top[:, i, :], in_=penal[i % len(penal)]).then_inc(pen_used, 1)
            dve.drain()
            dve.tensor_tensor(pick, pick, top, ALU.mult)
            dve.drain()
            dve.tensor_reduce(thr[:], pick, AX.X, ALU.add)
            dve.drain()
            dve.tensor_tensor(span[:], span[:], thr[:], ALU.add)
            dve.drain()
            dve.scalar_tensor_tensor(fits[:], span[:], 0.0, fits[:], ALU.is_gt, ALU.mult)
            dve.drain()
            dve.tensor_reduce(proved[:], fits[:], AX.X, ALU.add)
            dve.drain().then_inc(proved_sb, 1)
            dve.wait_ge(proved_ps, 1)
            dve.tensor_copy(proved_i[:], ps[0:1, 7, 0:1])
            dve.drain()
            n_proved = dve.value_load(proved_i[0:1, 0:1], min_val=0, max_val=TOKENS)
            with dve.If(n_proved < TOKENS):
                with dve.Fori(0, T) as i:
                    dve.tensor_copy(xnT[:, 0, :], sim[:, bass.ds(i, 1), :].rearrange("p a n -> p (a n)"))
                    dve.drain()
                    with dve.Fori(0, (TOPK - 1) // WINDOW):
                        dve.max(out=work[:], in_=xnT[:, 0, :])
                        dve.drain()
                        dve.match_replace(out=xnT[:, 0, :], in_to_replace=work[:], in_values=xnT[:, 0, :],
                                          imm_value=LOWEST)
                        dve.drain()
                    dve.max(out=work[:], in_=xnT[:, 0, :])
                    dve.drain()
                    dve.tensor_copy(thr[:, bass.ds(i, 1)], work[:, (TOPK - 1) % WINDOW:(TOPK - 1) % WINDOW + 1])
                    dve.drain()
            with dve.Else():
                dve.drain()
            dve.drain()

            def norm(b):
                u = b % 2
                dve.wait_ge(x1_rstd, b + 1)
                dve.scalar_tensor_tensor(xn_bias[:, u, :], xn_scale[:, u, :], -1.0, mv1[:, u, :, 0], ALU.mult, ALU.mult)
                dve.drain()
                if b >= 1:
                    dve.wait_ge(xn_out, 16 * b)
                    dve.wait_ge(xnT_ps, BT * b)
                else:
                    dve.wait_ge(pad_out, 16)
                for t in range(BT):
                    dve.tensor_scalar(xnb[:, t, :], xb[:, u, t, :], xn_scale[:, u, t:t + 1], xn_bias[:, u, t:t + 1],
                                      ALU.mult, ALU.add).then_inc(xn_done, 1)

            def mask(b, t):
                i = b * BT + t
                dve.wait_ge(sig_done, i + 1)
                dve.scalar_tensor_tensor(ab[:, b % 2, t, :], sim[:, i, :], thr[:, i:i + 1], ab[:, b % 2, t, :],
                                         ALU.is_ge, ALU.mult).then_inc(a_done, 1)

            hot_g = hot.rearrange("p i k e -> p (i k) e")
            hot_wg = hot_w.rearrange("p i k e -> p (i k) e")

            def best_two(b):
                tiles = slice(b * BT, (b + 1) * BT)
                groups = slice(b * BT * PICKS, (b + 1) * BT * PICKS)
                n = BT * PICKS
                dve.wait_ge(log_sb, b + 1)
                for i in range(b * BT, (b + 1) * BT):
                    dve.max(out=best[:, i, :], in_=logits[:, i, :])
                dve.drain()
                dve.tensor_tensor(gap[:, tiles], best[:, tiles, 0], best[:, tiles, 1], ALU.subtract)
                for i in range(b * BT, (b + 1) * BT):
                    dve.max_index(out=best_i[:, i, :], in_max=best[:, i, :], in_values=logits[:, i, :])
                dve.drain()
                dve.tensor_copy(idx_f[:, tiles], best_i[:, tiles, 0:PICKS])
                dve.drain()
                dve.tensor_tensor(hot_g[:, groups], iota_e[:, None, :].to_broadcast([P, n, E]),
                                  idx_f[:, tiles].rearrange("p i k -> p (i k)")[:, :, None].to_broadcast([P, n, E]),
                                  ALU.is_equal)
                dve.drain()
                dve.tensor_tensor(member[:, b * BT * E:(b + 1) * BT * E].rearrange("p (i e) -> p i e", i=BT),
                                  hot[:, tiles, 0, :], hot[:, tiles, 1, :], ALU.add)
                if b == BATCH - 1:
                    dve.drain().then_inc(member_ok, 1)
                dve.tensor_tensor(hot_wg[:, groups], hot_g[:, groups], alpha_bc[:, None, :].to_broadcast([P, n, E]),
                                  ALU.mult)
                dve.drain()
                dve.tensor_reduce(w_tok_g[:, groups], hot_wg[:, groups], AX.X, ALU.add)

            for b in range(2):
                for t in range(BT):
                    mask(b, t)
            for b in range(BATCH):
                u = b % 2
                for t in range(BT):
                    i = b * BT + t
                    dve.wait_ge(xa_done, i + 1)
                    dve.wait_ge(x1_ps, i + 1)
                    dve.tensor_tensor(xb[:, u, t, :], xb[:, u, t, :], ps[:, t, :], ALU.add)
                    dve.drain().then_inc(x1_sb, 1)
                    dve.bn_stats(stat1[:, t, :], xb[:, u, t, :])
                    if b >= 1 and t == 0:
                        norm(b - 1)
                    if 1 <= b < BATCH - 1:
                        mask(b + 1, t)
                dve.drain()
                for t in range(BT):
                    dve.bn_aggr(mv1[:, u, t, :], stat1[:, t, :])
                dve.drain().then_inc(x1_var, 1)
            best_two(0)
            norm(BATCH - 1)
            for b in range(1, BATCH):
                best_two(b)
            dve.drain().then_inc(gap_ok, 1)
            dve.wait_ge(score_ok, 1)
            dve.scalar_tensor_tensor(w_tok_g, score[:].rearrange("p i k -> p (i k)"), tanh_gf, w_tok_g,
                                     ALU.mult, ALU.mult)
            dve.wait_ge(rank_ps, 1)
            dve.tensor_copy(totals, ps[:, 5, 0:T * E].rearrange("p (i e) -> p e i", i=T))
            dve.drain()
            tot_f = totals.rearrange("p e i -> p (e i)")
            run_f = running.rearrange("p e i -> p (e i)")
            dve.tensor_tensor_scan(out=run_f, data0=ones[:], data1=tot_f, initial=0.0, op0=ALU.mult, op1=ALU.add)
            dve.drain()
            dve.tensor_tensor(start_e[:], running[:, :, 0], totals[:, :, 0], ALU.subtract)
            dve.drain()
            dve.tensor_tensor(count_e[:], running[:, :, T - 1], start_e[:], ALU.subtract)
            dve.drain()
            dve.tensor_tensor(run_f, run_f, tot_f, ALU.subtract)
            dve.tensor_tensor(tiles_cmp, count_e[:, :, None].to_broadcast([P, E, T]),
                              tile_starts[:, None, :].to_broadcast([P, E, T]), ALU.is_gt)
            dve.drain()
            dve.tensor_reduce(tiles_e[:], tiles_cmp, AX.X, ALU.add)
            dve.drain()
            dve.tensor_tensor_scan(out=tiles_end[:], data0=ones[:, 0:E], data1=tiles_e[:], initial=0.0,
                                   op0=ALU.mult, op1=ALU.add)
            dve.drain()
            dve.tensor_tensor(base_e[:], tiles_end[:], tiles_e[:], ALU.subtract)
            dve.drain()
            dve.scalar_tensor_tensor(base_e[:], base_e[:], float(P), start_e[:], ALU.mult, ALU.subtract)
            dve.drain()
            dve.tensor_tensor(place, running.rearrange("p e i -> p i e"),
                              base_e[:, None, :].to_broadcast([P, T, E]), ALU.add)
            dve.drain()
            dve.tensor_tensor(place, place, ps[:, 4, 0:T * E].rearrange("p (i e) -> p i e", i=T), ALU.add)
            dve.drain()
            for k in range(PICKS):
                dve.tensor_tensor(hot_w[:, :, k, :], hot[:, :, k, :], place, ALU.mult)
            dve.drain()
            dve.tensor_reduce(pos[:], hot_wg, AX.X, ALU.add)
            dve.drain()
            dve.tensor_scalar(pos_j[:], pos[:], 1.0 / P, -(P - 1) / (2.0 * P), ALU.mult, ALU.add)
            dve.drain()
            dve.tensor_copy(pos_jf[:], pos_j[:])
            dve.scalar_tensor_tensor(pos_qf[:], pos_j[:], -float(P), pos[:], ALU.mult, ALU.add)
            dve.drain()
            for c in range(CHUNKS):
                g = chunk[c]
                shape = [P, GROUPS // CHUNKS, TILES]
                dve.tensor_tensor(tile_hot[:, g, :], iota_j[:, None, :].to_broadcast(shape),
                                  pos_jf[:, g, None].to_broadcast(shape), ALU.is_equal)
                dve.drain().then_inc(tile_ok, 1)
                rows = [P, GROUPS // CHUNKS, P]
                dve.tensor_tensor(slot_hot[:, g, :], iota_q[:, None, :].to_broadcast(rows),
                                  pos_qf[:, g, None].to_broadcast(rows), ALU.is_equal)
                dve.drain().then_inc(hot_ok, 1)
            dve.tensor_tensor(exp_cmp, tiles_end[0:1, None, :].to_broadcast([1, TILES, E]),
                              iota_j[0:1, :, None].to_broadcast([1, TILES, E]), ALU.is_le)
            dve.drain()
            dve.tensor_reduce(exp_f[:], exp_cmp, AX.X, ALU.add)
            dve.drain()
            dve.tensor_scalar(exp_i[:], exp_f[:], float(E - 1), None, ALU.min)
            dve.tensor_copy(used_i[:], tiles_end[0:1, E - 1:E])
            dve.drain().then_inc(route_ok, 1)
            dve.wait_ge(table_ps, 1)
            dve.tensor_copy(table, ps[:, 7, 0:2 * TILES].rearrange("p (v j) -> p v j", v=2))
            dve.drain()
            dve.tensor_scalar(src_idx[:], table[:, 0, :], -1.0, 0.0, ALU.add, ALU.max)
            dve.drain().then_inc(src_ok, 1)
            dve.tensor_scalar(empty, table[:, 0, :], 0.0, pad_row_1[:, 0:1], ALU.is_equal, ALU.mult)
            dve.tensor_copy(w_slot[:], table[:, 1, :])
            dve.drain()
            dve.scalar_tensor_tensor(dst_idx[:], table[:, 0, :], -1.0, empty, ALU.add, ALU.add)
            dve.drain().then_inc(dst_ok, 1)

            dve.wait_ge(b2_in_s, 16)

            def hidden(j, u):
                dve.wait_ge(hid_ps, j + 1)
                dve.tensor_copy(hid[u], ps[:, 2 + u, :]).then_inc(hid_sb, 1)

            def result(j, u):
                e = dve.value_load(exp_i[0:1, bass.ds(j, 1)], min_val=0, max_val=E - 1)
                dve.wait_ge(y_ps, j + 1)
                dve.tensor_tensor(yb[u], ps[:, 6 + u, :], b2_bc[:, bass.ds(e, 1), :].rearrange("p a n -> p (a n)"),
                                  ALU.add)
                dve.drain().then_inc(y_sb, 1)
                dve.wait_ge(rows_added, j + 1)
                dve.tensor_scalar(ys[u], yb[u], w_slot[:, bass.ds(j, 1)], None, ALU.mult).then_inc(ys_ready, 1)

            def transposed(j, u):
                dve.wait_ge(xgT_ps, j + 1)
                dve.tensor_copy(xgT[u], ps[:, u, :]).then_inc(xgT_sb, 1)

            def evacuate(first, tiles):
                transposed(first, 0)
                hidden(first, 0)
                transposed(first + 1, 1)
                looped = (tiles - 2) // 2
                if looped:
                    with dve.Fori(first // 2, first // 2 + looped) as jj:
                        for u in range(2):
                            j = jj * 2 + u
                            hidden(j + 1, 1 - u)
                            transposed(j + 2, u)
                            result(j, u)
                for j in range(first + looped * 2, first + tiles):
                    if j + 1 < first + tiles:
                        hidden(j + 1, (j + 1) % 2)
                    if j + 2 < first + tiles:
                        transposed(j + 2, j % 2)
                    result(j, j % 2)

            evacuate(0, MAIN_TILES)
            used = dve.value_load(used_i[0:1, 0:1], min_val=0, max_val=TILES)
            with dve.If(used > MAIN_TILES):
                evacuate(MAIN_TILES, TILES - MAIN_TILES)
            with dve.Else():
                dve.drain()

        @block.tensor
        def _(pe):
            def keep_busy(matmuls):
                with pe.Fori(0, matmuls // 4):
                    for _ in range(4):
                        pe.matmul(ps[:, 6, 0:P], ones_b[:], ones_b[:], start=True, stop=True)

            pe.wait_ge(consts, 2)
            keep_busy(BUSY_LOADS)
            pe.wait_ge(qk_in, 32)
            pe.wait_ge(b1_in_s, 16)
            pe.transpose(ps[:, 3, 0:C], wq, ident[:])
            pe.transpose(ps[:, 3, C:2 * C], wk, ident[:])
            pe.transpose(ps[:, 3, 2 * C:2 * C + E * IB], b1_rows, ident[0:E * IB, 0:E * IB]).then_inc(wT_ps, 1)
            pe.wait_ge(wT_sb, 1)
            def turn_context(b):
                pe.wait_ge(ctx_in_s[b], 16)
                for t in range(BT):
                    mm = pe.transpose(ps[:, b % 2, t * P:(t + 1) * P], ctx_b[b][:, t * C:(t + 1) * C], ident[:])
                mm.then_inc(ctxT_ps, 1)

            turn_context(0)
            for b in range(BATCH):
                if b + 1 < BATCH:
                    turn_context(b + 1)
                pe.wait_ge(ctxT_sb, b + 1)
                if b >= 2:
                    pe.wait_ge(qk_sb, 2 * (b - 1))
                pe.matmul(ps[:, 2 + b % 2, :], wqT, ctxT[b], start=True, stop=True).then_inc(q_ps, 1)
                pe.matmul(ps[:, 4 + b % 2, :], wkT, ctxT[b], start=True, stop=True).then_inc(k_ps, 1)
            for i in range(T):
                b, t = i // BT, i % BT
                if t == 0:
                    pe.wait_ge(qk_sb, 2 * (b + 1))
                if i >= 4:
                    pe.wait_ge(sim_sb, i - 3)
                pe.matmul(ps[:, SIM_BANKS[i % 4], :], qT[b][:, t * P:(t + 1) * P], kT[b], start=True,
                          stop=True).then_inc(sim_ps, 1)
            pe.wait_ge(sim_sb, T)
            pe.wait_ge(proved_sb, 1)
            pe.matmul(ps[0:1, 7, 0:1], proved[:], ones[:, 0:1], start=True, stop=True).then_inc(proved_ps, 1)
            keep_busy(BUSY_PROOF)
            pe.wait_ge(const_in, 16)
            pe.wait_ge(coef_ok, 1)

            def add_adjacency(b):
                u = b % 2
                pe.wait_ge(a_done, BT * (b + 1))
                for t in range(BT):
                    if b >= 1:
                        pe.wait_ge(x1_sb, (b - 1) * BT + t + 1)
                    pe.matmul(ps[:, t, :], ident_a[:], ab[:, u, t, :], start=True, stop=False)
                    for q in range(BT):
                        mm = pe.matmul(ps[:, t, q * P:(q + 1) * P], ab[:, u, q, t * P:(t + 1) * P], ident_a[:],
                                       start=False, stop=(q == BT - 1))
                    mm.then_inc(x1_ps, 1)

            def gate(b):
                def turn(t):
                    i = b * BT + t
                    pe.wait_ge(xn_done, i + 1)
                    if i >= 2:
                        pe.wait_ge(xnT_sb, i - 1)
                    for k in range(KB):
                        mm = pe.transpose(ps[:, 4 + t % 2, k * P:(k + 1) * P], xnb[:, t, k * P:(k + 1) * P], ident[:])
                    mm.then_inc(xnT_ps, 1)

                turn(0)
                turn(1)
                if b >= 1:
                    pe.wait_ge(logT_sb, b)
                for t in range(BT):
                    pe.wait_ge(xnT_sb, b * BT + t + 1)
                    for k in range(KB):
                        mm = pe.matmul(ps[0:E, 6, t * P:(t + 1) * P], gate_w[:, k, :], xnT[:, t % 2, k * P:(k + 1) * P],
                                       start=(k == 0), stop=(k == KB - 1))
                    mm.then_inc(gate_ps, 1)
                    if t + 2 < BT:
                        turn(t + 2)

            def turn_logits(b):
                pe.wait_ge(logT_sb, b + 1)
                if b >= 1:
                    pe.wait_ge(log_sb, b)
                for t in range(BT):
                    mm = pe.transpose(ps[:, 7, t * E:(t + 1) * E], logT(b)[:, t * P:(t + 1) * P], ident[0:E, 0:E])
                mm.then_inc(log_ps, 1)

            add_adjacency(0)
            for b in range(BATCH):
                if b + 1 < BATCH:
                    add_adjacency(b + 1)
                if b >= 1:
                    turn_logits(b - 1)
                gate(b)
            turn_logits(BATCH - 1)
            pe.wait_ge(member_ok, 1)
            pe.matmul(ps[:, 4, 0:T * E], before[:], member[:], start=True, stop=True)
            pe.matmul(ps[:, 5, 0:T * E], ones_b[:], member[:], start=True, stop=True).then_inc(rank_ps, 1)
            keep_busy(BUSY_SLOTS)
            for c in range(CHUNKS):
                pe.wait_ge(hot_ok, c + 1)
                pe.wait_ge(value_ok, c + 1)
                for g in range(chunk[c].start, chunk[c].stop):
                    mm = pe.matmul(ps[:, 7, 0:2 * TILES], slot_hot[:, g, :],
                                   tile_val[:, g].rearrange("p v j -> p (v j)"), start=(g == 0), stop=(g == GROUPS - 1))
            mm.then_inc(table_ps, 1)

            keep_busy(BUSY_GATHER)
            pe.wait_ge(fc1_in, 16 * E)
            pe.wait_ge(fc2_in, 16 * E)
            pe.wait_ge(route_ok, 1)

            def expert(j):
                return pe.value_load(exp_i[0:1, bass.ds(j, 1)], min_val=0, max_val=E - 1)

            def w_block(e, m, k):
                return weights[:, bass.ds(e, 1), m, k, :].rearrange("p a n -> p (a n)")

            def turn_rows(u, arrivals):
                pe.wait_ge(gathered[u], arrivals)
                for k in range(KB):
                    mm = pe.transpose(ps[:, u, k * P:(k + 1) * P], xg[u][:, k * P:(k + 1) * P], ident[:])
                mm.then_inc(xgT_ps, 1)

            def layer1(j, u):
                e = expert(j)
                pe.wait_ge(xgT_sb, j + 1)
                for k in range(KB):
                    mm = pe.matmul(ps[:, 2 + u, :], xgT[u][:, k * P:(k + 1) * P], w_block(e, 0, k), start=(k == 0),
                                   stop=(k == KB - 1))
                mm.then_inc(hid_ps, 1)

            def turn_hidden(j, u):
                pe.wait_ge(hid_sb, j + 1)
                for i in range(IB):
                    mm = pe.transpose(ps[:, 4 + u, i * P:(i + 1) * P], hid[u][:, i * P:(i + 1) * P], ident[:])
                mm.then_inc(hidT_ps, 1)

            def layer2(j, u):
                e = expert(j)
                pe.wait_ge(gelu_sb, j + 1)
                pe.wait_ge(y_sb, j + 1)
                for i in range(IB):
                    mm = pe.matmul(ps[:, 6 + u, :], act_t[u][:, i * P:(i + 1) * P], w_block(e, 1, i), start=(i == 0),
                                   stop=(i == IB - 1))
                mm.then_inc(y_ps, 1)

            def feed_forward(first, tiles):
                turn_rows(0, 16 * (first // 2 + 1))
                layer1(first, 0)
                turn_rows(1, 16 * (first // 2 + 1))
                looped = (tiles - 2) // 2
                if looped:
                    with pe.Fori(first // 2, first // 2 + looped) as jj:
                        for u in range(2):
                            j = jj * 2 + u
                            turn_hidden(j, u)
                            layer1(j + 1, 1 - u)
                            turn_rows(u, 16 * jj + 32)
                            layer2(j, u)
                for j in range(first + looped * 2, first + tiles):
                    turn_hidden(j, j % 2)
                    if j + 1 < first + tiles:
                        layer1(j + 1, (j + 1) % 2)
                    if j + 2 < first + tiles:
                        turn_rows(j % 2, 16 * (j // 2 + 2))
                    layer2(j, j % 2)

            feed_forward(0, MAIN_TILES)
            used = pe.value_load(used_i[0:1, 0:1], min_val=0, max_val=TILES)
            with pe.If(used > MAIN_TILES):
                feed_forward(MAIN_TILES, TILES - MAIN_TILES)
            with pe.Else():
                pe.drain()


_INS = ["x", "ctx_512", "g_xattn", "g_ffn", "L0_xattn_Wq", "L0_xattn_Wk", "L0_xattn_gamma_raw", "L0_ffn_gate_w",
        "L0_ffn_fc1_w", "L0_ffn_fc1_b", "L0_ffn_fc2_w", "L0_ffn_fc2_b", "L0_ffn_alpha"]


def kernel(**inputs):
    import concourse.bacc as bacc
    from concourse.bass_utils import run_bass_kernel_spmd as run

    nc = bacc.Bacc("TRN2", target_bir_lowering=False, num_devices=1, dynamic_dma_scratch_size=8192)
    arrays, args = {}, []
    for name in _INS:
        a = np.ascontiguousarray(inputs[name])
        if name in ("x", "ctx_512"):
            a = a.reshape(TOKENS, -1)
        if a.ndim == 0:
            a = a.reshape(1)
        arrays[f"in_{name}"] = a
        args.append(nc.dram_tensor(f"in_{name}", a.shape, mybir.dt.from_np(a.dtype), kind="ExternalInput").ap())
    xn_rows = nc.dram_tensor("xn_rows", (TOKENS, D), F32, kind="Internal").ap()
    out_rows = nc.dram_tensor("out_rows", (TOKENS + P, D), F32, kind="ExternalOutput").ap()
    build(nc, *args, xn_rows, out_rows)
    r = run(nc, [arrays], core_ids=[0])
    return r.results[0]["out_rows"][:TOKENS].reshape(BATCH, SEQ, D)
```
